# Optimizing a Trainium2 kernel written in Bass

```python
import numpy as np
import jax
import jax.numpy as jnp

def _softmax(x, axis=-1):
    return jax.nn.softmax(x, axis=axis)

def _gelu(x):
    return jax.nn.gelu(x, approximate=True)

def _silu(x):
    return jax.nn.silu(x)

def _sigmoid(x):
    return jax.nn.sigmoid(x)

def _layernorm(x, axis=-1, eps=1e-05):
    m = jnp.mean(x, axis=axis, keepdims=True)
    v = jnp.var(x, axis=axis, keepdims=True)
    return (x - m) / jnp.sqrt(v + eps)

def _scatter_add(tgt, idx, src, axis=0):
    return tgt.at[idx].add(src)

def _segment_sum(src, seg, n):
    return jax.ops.segment_sum(src, seg, n)
kernel_name = 'mk_adj_ffn_d1_adj_r2_b0a72b'

def setup_inputs(seed: int=0):
    np.random.seed(seed)
    _w = jnp.asarray

    def _rec_inputs():
        import jax
        import jax.numpy as jnp
        _gk = jax.random.key(seed)
        x = -0.0002928 + 1 * jax.random.normal(jax.random.fold_in(_gk, 1), (64, 128, 256), jnp.float32)
        _a = jax.random.bernoulli(jax.random.fold_in(_gk, 2), 0.0625, (64, 128, 128))
        _a = jnp.logical_or(_a, jnp.swapaxes(_a, -1, -2))
        _a = jnp.logical_or(_a, jnp.eye(128, dtype=bool))
        _af = _a.astype(jnp.float32)
        _af = _af * jax.random.uniform(jax.random.fold_in(_gk, 3), (64, 128, 128), jnp.float32, 0.05, 1)
        adj = _af
        return (x, adj)
    x, adj = _rec_inputs()

    def _L0_gnn_setup():
        import jax, jax.numpy as jnp
        import numpy as np
        B, N, DIN, DOUT, K = (4, 1024, 256, 256, 3)
        key = jax.random.key(seed)
        ks = jax.random.split(key, 8)
        X = jax.random.normal(ks[0], (B, N, DIN), dtype=jnp.float32)
        A = jax.random.uniform(ks[1], (B, N, N), dtype=jnp.float32)
        Wv = jax.random.normal(ks[2], (DIN, DOUT), dtype=jnp.float32) * 0.02
        bv = jax.random.normal(ks[3], (DOUT,), dtype=jnp.float32) * 0.02
        aw = jax.random.normal(ks[4], (2 * DOUT, 1), dtype=jnp.float32) * 0.05
        ab = jax.random.normal(ks[5], (1,), dtype=jnp.float32) * 0.05
        Wk = jax.random.normal(ks[6], (K, DIN, DOUT), dtype=jnp.float32) * 0.02
        bk = jax.random.normal(ks[7], (K, DOUT), dtype=jnp.float32) * 0.02
        return {'X': X, 'A': A, 'Wv': Wv, 'bv': bv, 'aw': aw, 'ab': ab, 'Wk': Wk, 'bk': bk}
    _L0_gnn_all = _L0_gnn_setup()
    _L0_gnn_in = {k: v for k, v in _L0_gnn_all.items() if k in ('Wv', 'bv', 'aw', 'ab', 'Wk', 'bk')}
    del _L0_gnn_all

    def _L0_ffn_setup():
        import jax, jax.numpy as jnp
        import numpy as np
        D_MODEL, D_STATE, D_CONV, D_INPUT, D_OUTPUT = (512, 16, 4, 256, 256)
        EXPAND = 2
        D_INNER = EXPAND * D_MODEL
        DT_RANK = (D_MODEL + 15) // 16
        B, L = (4, 1024)

        def _mamba(x, W_in, conv_w, conv_b, W_xproj, W_dt, b_dt, A_log, Dp, W_out):
            xz = jnp.einsum('bld,ed->ble', x, W_in)
            u, z = jnp.split(xz, 2, axis=-1)
            u_pad = jnp.pad(u, ((0, 0), (D_CONV - 1, 0), (0, 0)))
            u = sum((u_pad[:, k:k + u.shape[1], :] * conv_w[:, k] for k in range(D_CONV))) + conv_b
            u = jax.nn.silu(u)
            dbc = jnp.einsum('bld,ed->ble', u, W_xproj)
            dt, B_ssm, C_ssm = jnp.split(dbc, [DT_RANK, DT_RANK + D_STATE], axis=-1)
            delta = jax.nn.softplus(jnp.einsum('blr,dr->bld', dt, W_dt) + b_dt)
            A = -jnp.exp(A_log)

            def step(h, ins):
                d_t, B_t, C_t, u_t = ins
                dA = jnp.exp(d_t[..., None] * A)
                h = dA * h + (d_t * u_t)[..., None] * B_t[:, None, :]
                y_t = jnp.einsum('bds,bs->bd', h, C_t)
                return (h, y_t)
            h0 = jnp.zeros((u.shape[0], D_INNER, D_STATE), u.dtype)
            xs = (delta.transpose(1, 0, 2), B_ssm.transpose(1, 0, 2), C_ssm.transpose(1, 0, 2), u.transpose(1, 0, 2))
            _, y = jax.lax.scan(step, h0, xs)
            y = y.transpose(1, 0, 2) + u * Dp
            y = y * jax.nn.silu(z)
            return jnp.einsum('bld,ed->ble', y, W_out)
        key = jax.random.key(seed)
        ks = jax.random.split(key, 16)
        s = lambda fan_in: 1.0 / np.sqrt(fan_in)
        inp = {'x': jax.random.normal(ks[0], (B, L, D_INPUT), jnp.float32), 'W_fc1': jax.random.normal(ks[1], (D_MODEL, D_INPUT), jnp.float32) * s(D_INPUT), 'b_fc1': jnp.zeros((D_MODEL,), jnp.float32), 'W_in': jax.random.normal(ks[2], (2 * D_INNER, D_MODEL), jnp.float32) * s(D_MODEL), 'conv_w': jax.random.normal(ks[3], (D_INNER, D_CONV), jnp.float32) * s(D_CONV), 'conv_b': jnp.zeros((D_INNER,), jnp.float32), 'W_xproj': jax.random.normal(ks[4], (DT_RANK + 2 * D_STATE, D_INNER), jnp.float32) * s(D_INNER), 'W_dt': jax.random.normal(ks[5], (D_INNER, DT_RANK), jnp.float32) * s(DT_RANK), 'b_dt': jax.random.uniform(ks[6], (D_INNER,), jnp.float32, -4.0, -2.0), 'A_log': jnp.log(jnp.broadcast_to(jnp.arange(1, D_STATE + 1, dtype=jnp.float32), (D_INNER, D_STATE))), 'D': jnp.ones((D_INNER,), jnp.float32), 'W_out': jax.random.normal(ks[7], (D_MODEL, D_INNER), jnp.float32) * s(D_INNER), 'W_fc2': jax.random.normal(ks[8], (D_OUTPUT, D_MODEL), jnp.float32) * s(D_MODEL), 'b_fc2': jnp.zeros((D_OUTPUT,), jnp.float32)}
        return inp
    _L0_ffn_all = _L0_ffn_setup()
    _L0_ffn_in = {k: v for k, v in _L0_ffn_all.items() if k in ('W_fc1', 'b_fc1', 'W_in', 'conv_w', 'conv_b', 'W_xproj', 'W_dt', 'b_dt', 'A_log', 'D', 'W_out', 'W_fc2', 'b_fc2')}
    del _L0_ffn_all
    return {'x': x, 'adj': adj, 'L0_gnn_Wv': _L0_gnn_in['Wv'], 'L0_gnn_bv': _L0_gnn_in['bv'], 'L0_gnn_aw': _L0_gnn_in['aw'], 'L0_gnn_ab': _L0_gnn_in['ab'], 'L0_gnn_Wk': _L0_gnn_in['Wk'], 'L0_gnn_bk': _L0_gnn_in['bk'], 'L0_ffn_W_fc1': _L0_ffn_in['W_fc1'], 'L0_ffn_b_fc1': _L0_ffn_in['b_fc1'], 'L0_ffn_W_in': _L0_ffn_in['W_in'], 'L0_ffn_conv_w': _L0_ffn_in['conv_w'], 'L0_ffn_conv_b': _L0_ffn_in['conv_b'], 'L0_ffn_W_xproj': _L0_ffn_in['W_xproj'], 'L0_ffn_W_dt': _L0_ffn_in['W_dt'], 'L0_ffn_b_dt': _L0_ffn_in['b_dt'], 'L0_ffn_A_log': _L0_ffn_in['A_log'], 'L0_ffn_D': _L0_ffn_in['D'], 'L0_ffn_W_out': _L0_ffn_in['W_out'], 'L0_ffn_W_fc2': _L0_ffn_in['W_fc2'], 'L0_ffn_b_fc2': _L0_ffn_in['b_fc2']}

def reference(x, adj, L0_gnn_Wv, L0_gnn_bv, L0_gnn_aw, L0_gnn_ab, L0_gnn_Wk, L0_gnn_bk, L0_ffn_W_fc1, L0_ffn_b_fc1, L0_ffn_W_in, L0_ffn_conv_w, L0_ffn_conv_b, L0_ffn_W_xproj, L0_ffn_W_dt, L0_ffn_b_dt, L0_ffn_A_log, L0_ffn_D, L0_ffn_W_out, L0_ffn_W_fc2, L0_ffn_b_fc2):
    import jax
    import jax.numpy as jnp

    def _L0_gnn_ref(X, A, Wv, bv, aw, ab, Wk, bk):
        import jax, jax.numpy as jnp
        import numpy as np
        B, N, DIN, DOUT, K = (4, 1024, 256, 256, 3)
        d = Wv.shape[1]
        Xw = X @ Wv + bv
        sj = Xw @ aw[:d, 0]
        si = Xw @ aw[d:, 0]
        e = jax.nn.leaky_relu(sj[:, None, :] + si[:, :, None] + ab[0], negative_slope=0.2)
        alpha_matrix = A * jnp.exp(e)
        transition = alpha_matrix / (jnp.sum(alpha_matrix, axis=-1, keepdims=True) + 1e-12)
        H = jnp.zeros(X.shape[:-1] + (d,), dtype=X.dtype)
        Xk = X
        for k in range(Wk.shape[0]):
            H = H + Xk @ Wk[k] + bk[k]
            Xk = jnp.einsum('bij,bjd->bid', transition, Xk)
        return jax.nn.relu(H)

    def _L0_ffn_ref(x, W_fc1, b_fc1, W_in, conv_w, conv_b, W_xproj, W_dt, b_dt, A_log, D, W_out, W_fc2, b_fc2):
        import jax, jax.numpy as jnp
        import numpy as np
        D_MODEL, D_STATE, D_CONV, D_INPUT, D_OUTPUT = (512, 16, 4, 256, 256)
        EXPAND = 2
        D_INNER = EXPAND * D_MODEL
        DT_RANK = (D_MODEL + 15) // 16
        B, L = (4, 1024)

        def _mamba(x, W_in, conv_w, conv_b, W_xproj, W_dt, b_dt, A_log, Dp, W_out):
            xz = jnp.einsum('bld,ed->ble', x, W_in)
            u, z = jnp.split(xz, 2, axis=-1)
            u_pad = jnp.pad(u, ((0, 0), (D_CONV - 1, 0), (0, 0)))
            u = sum((u_pad[:, k:k + u.shape[1], :] * conv_w[:, k] for k in range(D_CONV))) + conv_b
            u = jax.nn.silu(u)
            dbc = jnp.einsum('bld,ed->ble', u, W_xproj)
            dt, B_ssm, C_ssm = jnp.split(dbc, [DT_RANK, DT_RANK + D_STATE], axis=-1)
            delta = jax.nn.softplus(jnp.einsum('blr,dr->bld', dt, W_dt) + b_dt)
            A = -jnp.exp(A_log)

            def step(h, ins):
                d_t, B_t, C_t, u_t = ins
                dA = jnp.exp(d_t[..., None] * A)
                h = dA * h + (d_t * u_t)[..., None] * B_t[:, None, :]
                y_t = jnp.einsum('bds,bs->bd', h, C_t)
                return (h, y_t)
            h0 = jnp.zeros((u.shape[0], D_INNER, D_STATE), u.dtype)
            xs = (delta.transpose(1, 0, 2), B_ssm.transpose(1, 0, 2), C_ssm.transpose(1, 0, 2), u.transpose(1, 0, 2))
            _, y = jax.lax.scan(step, h0, xs)
            y = y.transpose(1, 0, 2) + u * Dp
            y = y * jax.nn.silu(z)
            return jnp.einsum('bld,ed->ble', y, W_out)
        h = jnp.einsum('bli,oi->blo', x, W_fc1) + b_fc1
        h = _mamba(h, W_in, conv_w, conv_b, W_xproj, W_dt, b_dt, A_log, D, W_out)
        return jnp.einsum('bld,od->blo', h, W_fc2) + b_fc2
    x = x + _L0_gnn_ref(_layernorm(x, axis=-1), adj, L0_gnn_Wv, L0_gnn_bv, L0_gnn_aw, L0_gnn_ab, L0_gnn_Wk, L0_gnn_bk)
    x = x + _L0_ffn_ref(_layernorm(x, axis=-1), L0_ffn_W_fc1, L0_ffn_b_fc1, L0_ffn_W_in, L0_ffn_conv_w, L0_ffn_conv_b, L0_ffn_W_xproj, L0_ffn_W_dt, L0_ffn_b_dt, L0_ffn_A_log, L0_ffn_D, L0_ffn_W_out, L0_ffn_W_fc2, L0_ffn_b_fc2)
    return x

_drawn_inputs = setup_inputs


def setup_inputs(seed=0):
    import zlib

    import numpy as np

    out = dict(_drawn_inputs(seed))
    spreads = {'L0_ffn_b_fc1': (0.0, 0.1),
     'L0_ffn_conv_b': (0.0, 0.1),
     'L0_ffn_D': (1.0, 0.2),
     'L0_ffn_b_fc2': (0.0, 0.1)}
    factors = {'L0_gnn_Wv': 4.355, 'L0_gnn_bv': 22.658, 'L0_gnn_aw': 4.442}
    for name, (base, spread) in spreads.items():
        noise = np.random.default_rng([zlib.crc32(name.encode()), seed]).standard_normal(out[name].shape)
        drawn = base * np.exp(spread * noise) if base else spread * noise
        out[name] = jnp.asarray(drawn.astype(out[name].dtype))
    for name, factor in factors.items():
        out[name] = (out[name] * factor).astype(out[name].dtype)
    return out
```

```python
from contextlib import ExitStack

import concourse.bass as bass
from concourse import mybir

F32 = mybir.dt.float32
ALU = mybir.AluOpType
ACT = mybir.ActivationFunctionType

BATCH, L, DIM = 64, 128, 256
P = 128
INNER = 1024
STATE = 16
RANK = 32
TAPS = 4
HID = 512
HOPS = 3
PAIR = 2
GROUPS = BATCH // PAIR
T = PAIR * L
KC = DIM // P
HC = HID // P
J = INNER // P
PROJ = RANK + 2 * STATE
SU = 4
Q = STATE // SU
U = J * Q
SLOTS = 4
EPS_LN = 1e-5
EPS_ROW = 1e-12
EARLY = (27, 29)
LATE = (2, 5, 9, 13, 17, 21)
Z_STEPS = (2, 3, 5, 7, 11, 13, 14, 15)
ACT_LEAD, POOL_LAG, PE_LAG = 2, 0, 1


def build(nc, x, adjT, w_inT, w_fc1, w_out, w_fc2T, w_vT, aw, bv, ab, wk, bk, b_fc1, conv_w, conv_b,
          w_xT, w_dtT, b_dt, a_log, skip, b_fc2, ident_in, out):
    bc_dram = nc.dram_tensor("bc_dram", [2, 2, STATE * T], F32).ap()
    x1_dram = nc.dram_tensor("x1_dram", [GROUPS, P, PAIR * DIM], F32).ap()

    with ExitStack() as ctx:
        def sb(name, shape):
            return ctx.enter_context(nc.sbuf_tensor(name, shape, F32))

        def sem(name):
            return ctx.enter_context(nc.semaphore(name))

        wxz = sb("wxz", [P, KC, 2 * INNER])
        wo = sb("wo", [P, J, DIM])
        wx = sb("wx", [P, J, PROJ])
        rows = sb("rows", [P, INNER])
        wks = sb("wks", [P, HOPS, KC, DIM])
        wi_rep = sb("wi_rep", [P, KC, P])
        wj_rep = sb("wj_rep", [P, KC, P])
        ident = sb("ident", [P, P])
        decay = sb("decay", [P, J, STATE])
        bxz = sb("bxz", [P, 2 * J])
        chan = sb("chan", [P, TAPS + 3, J])
        c0 = sb("c0", [P, 1])
        one_col = sb("one_col", [P, 1])
        halfs = sb("halfs", [P, PAIR])
        ones3 = rows[32:32 + HOPS, PAIR * DIM:PAIR * DIM + P]
        one1 = rows[64:65, PAIR * DIM:PAIR * DIM + P]
        wdt = rows[0:RANK, :]
        bk_row = rows[32:32 + HOPS, 0:PAIR * DIM]
        bo_row = rows[64:65, 0:PAIR * DIM]

        bc = sb("bc", [P, 2, 2, STATE, T])
        delta = sb("delta", [P, 2, J, T])
        du = sb("du", [P, 2, J, T])
        u = sb("u", [P, 2, J, T])
        zs = sb("zs", [P, 2, J, T])
        xnT = sb("xnT", [P, 2, KC, T])

        dec = sb("dec", [P, SLOTS, SU, T])
        st = sb("st", [P, SLOTS, SU, T])
        upad = sb("upad", [P, 2, PAIR, L + TAPS - 1])
        yv = sb("yv", [P, 2, T])
        dbc = sb("dbc", [PROJ, T])

        xg = sb("xg", [P, PAIR, DIM])
        adjt = sb("adjt", [P, PAIR, L])
        xn = sb("xn", [P, PAIR, DIM])
        xT = sb("xT", [P, KC, T])
        att = sb("att", [P, PAIR, L])
        x1k = sb("x1k", [P, PAIR, DIM])
        u1T = sb("u1T", [P, KC, T])
        u2T = xn[:, :, :].rearrange("p b d -> p (b d)").rearrange("p (c t) -> p c t", c=KC)
        last_x = sb("last_x", [P, PAIR, DIM])
        bstat = sb("bstat", [P, PAIR, 6])
        mv = sb("mv", [P, PAIR, 2])
        veps = sb("veps", [P, PAIR])
        rstd = sb("rstd", [P, PAIR])
        rowsum = sb("rowsum", [P, PAIR])
        rinv = sb("rinv", [P, PAIR])

        def bank(name, shape):
            return ctx.enter_context(nc.psum_tensor(name, shape, F32))

        y_ps = bank("y_ps", [P, 2, 512])
        u_ps = bank("u_ps", [P, 2, T])
        z_ps = bank("z_ps", [P, 4, T])
        o_ps = bank("o_ps", [P, PAIR, DIM])
        g0 = bank("g0", [P, 512])
        g1 = bank("g1", [P, 512])
        x_ps = u_ps[0:PROJ, 0, :]
        d_ps = z_ps

        stage = bc[:, :, :, :, :].rearrange("p a b s t -> p (a b s t)")
        at = [0]

        def staged(*dims):
            n = 1
            for d in dims:
                n *= d
            v = stage[:, at[0]:at[0] + n]
            at[0] += n
            return v

        s_winT = staged(HC, 2 * INNER).rearrange("p (c e) -> p c e", c=HC)
        s_fc1 = staged(HC, DIM).rearrange("p (c e) -> p c e", c=HC)
        s_wout = staged(HC, INNER).rearrange("p (c e) -> p c e", c=HC)
        s_fc2T = staged(HC, DIM).rearrange("p (c e) -> p c e", c=HC)
        s_wvT = staged(KC, DIM).rearrange("p (c e) -> p c e", c=KC)
        s_awrep = staged(2 * KC, P).rearrange("p (c e) -> p c e", c=2 * KC)
        s_aw = staged(2 * KC)
        s_bv = staged(KC)
        s_bvrep = staged(KC, P).rearrange("p (c e) -> p c e", c=KC)
        s_bfc1 = staged(HC)
        s_ab = staged(1)
        s_alog = staged(J * STATE).rearrange("p (j s) -> p j s", j=J)

        names = """stands w_loaded memsets reps_made prep_mm prep_ev decay_exp decay_neg
        x_loaded adj_loaded stats aggr veps_made rstd_made normed transposed xT_made xnT_made
        e_mm e_biased e_leaky e_exp alpha_made u1_mm rowsum_eps rinv_made x1k_made u1T_mm u1T_made u2T_mm u2T_made
        h0_mm h_mm h0_made h_summed x1_made x1_stored x1_reloaded
        u_mm z_mm u_biased taps silu_u silu_z proj_mm dbc_made bc_stored b_loaded c_loaded
        dt_mm abs_relu soft_exp soft_ln delta_made du_made
        decays injected scanned c_times summed y_skip y_gated out_mm finished out_stored"""
        S = {n: sem(n) for n in names.split()}

        def wait(eng, name, value):
            if isinstance(value, int) and value <= 0:
                return
            eng.wait_ge(S[name], value)

        def stand(eng):
            eng.sem_inc(S["stands"], 1)

        def walk(eng, body, tail):
            body(eng, -2, 0, False, False, True)
            body(eng, -1, 1, False, True, True)
            body(eng, 0, 0, True, True, True)
            with eng.Fori(0, (GROUPS - 4) // 2) as i:
                body(eng, i * 2 + 1, 1, True, True, True)
                body(eng, i * 2 + 2, 0, True, True, True)
            body(eng, GROUPS - 3, 1, True, True, True)
            body(eng, GROUPS - 2, 0, True, True, False)
            body(eng, GROUPS - 1, 1, True, False, False)
            tail(eng, GROUPS, 0)

        def has_previous(k):
            return not (isinstance(k, int) and k <= 0)

        block = ctx.enter_context(nc.Block())

        @block.sync
        def _(sp):
            loads = [
                (s_wvT, w_vT), (s_aw, aw), (s_bv, bv), (s_ab[64:65, :], ab), (s_bfc1, b_fc1),
                (ident[:, :], ident_in), (wks[:, :, :, :], wk),
                (rows[32:32 + HOPS, 0:DIM], bk), (rows[32:32 + HOPS, DIM:2 * DIM], bk),
                (s_winT, w_inT), (s_fc1, w_fc1), (s_alog, a_log),
                (chan[:, 0:TAPS, :], conv_w), (chan[:, TAPS, :], conv_b), (chan[:, TAPS + 1, :], b_dt),
                (chan[:, TAPS + 2, :], skip),
                (wx[:, :, :], w_xT), (wdt, w_dtT), (s_wout, w_out), (s_fc2T, w_fc2T),
                (rows[64:65, 0:DIM], b_fc2), (rows[64:65, DIM:2 * DIM], b_fc2),
            ]
            for dst, src in loads:
                sp.dma_start(dst, src).then_inc(S["w_loaded"], 16)

            def body(sp, k, p, scan, dense, graph):
                g = k + 2
                if graph:
                    wait(sp, "x1_stored", 16 * g)
                    stand(sp)
                    wait(sp, "normed", 2 * g)
                    stand(sp)
                    sp.dma_start(xg[:, :, :], x[bass.ds(g * PAIR, PAIR)].rearrange("b t d -> t b d")
                                 if not isinstance(g, int) else
                                 x[g * PAIR:(g + 1) * PAIR].rearrange("b t d -> t b d")).then_inc(S["x_loaded"], 16)
                    wait(sp, "alpha_made", g)
                    stand(sp)
                    sp.dma_start(adjt[:, :, :], adjT[bass.ds(g * PAIR, PAIR)].rearrange("b j i -> j b i")
                                 if not isinstance(g, int) else
                                 adjT[g * PAIR:(g + 1) * PAIR].rearrange("b j i -> j b i")).then_inc(S["adj_loaded"], 16)
                if has_previous(k) and scan:
                    store_out(sp, k - 1)
                if scan:
                    wait(sp, "out_stored", 16 * k)
                    stand(sp)
                    sp.dma_start(last_x[:, :, :].rearrange("p b d -> p (b d)"),
                                 x1_dram[bass.ds(k, 1)].rearrange("a p n -> (a p) n")
                                 if not isinstance(k, int) else x1_dram[k]).then_inc(S["x1_reloaded"], 16)
                if dense:
                    g = k + 1
                    r = 1 - p
                    wait(sp, "dbc_made", g + 1)
                    stand(sp)
                    wait(sp, "b_loaded", 16 * g)
                    stand(sp)
                    sp.dma_start(bc_dram[r].rearrange("a (s t) -> (a s) t", s=STATE),
                                 dbc[RANK:PROJ, :]).then_inc(S["bc_stored"], 16)
                    wait(sp, "bc_stored", 16 * g + 16)
                    stand(sp)
                    wait(sp, "injected", U * (g - 1))
                    stand(sp)
                    sp.dma_start(bc[:, r, 0, :, :].rearrange("p s t -> p (s t)"),
                                 bc_dram[r, 0:1].to_broadcast([P, STATE * T])).then_inc(S["b_loaded"], 16)
                    wait(sp, "c_times", U * (g - 1))
                    stand(sp)
                    sp.dma_start(bc[:, r, 1, :, :].rearrange("p s t -> p (s t)"),
                                 bc_dram[r, 1:2].to_broadcast([P, STATE * T])).then_inc(S["c_loaded"], 16)
                if graph:
                    g = k + 2
                    wait(sp, "x1_made", g + 1)
                    stand(sp)
                    sp.dma_start(x1_dram[bass.ds(g, 1)].rearrange("a p n -> (a p) n")
                                 if not isinstance(g, int) else x1_dram[g],
                                 xg[:, :, :].rearrange("p b d -> p (b d)")).then_inc(S["x1_stored"], 16)

            def store_out(sp, g):
                wait(sp, "finished", g + 1)
                stand(sp)
                sp.dma_start(out[bass.ds(g * PAIR, PAIR)].rearrange("b t d -> t b d")
                             if not isinstance(g, int) else
                             out[g * PAIR:(g + 1) * PAIR].rearrange("b t d -> t b d"),
                             last_x[:, :, :]).then_inc(S["out_stored"], 16)

            def tail(sp, k, p):
                store_out(sp, k - 1)
                sp.wait_ge(S["out_stored"], 16 * GROUPS)
                sp.wait_ge(S["x1_stored"], 16 * GROUPS)
                sp.wait_ge(S["bc_stored"], 16 * GROUPS)

            walk(sp, body, tail)

        WLOADS = 22

        @block.gpsimd
        def _(pool):
            def body(pool, k, p, scan, dense, graph):
                r = 1 - p
                gd, gn = k + 1, k + 2
                for v in range(U):
                    if graph and v in (2, 26):
                        n = 2 * gn + (v == 26)
                        wait(pool, "aggr", n + 1)
                        stand(pool)
                        nc.gpsimd.tensor_scalar(veps[:, :], mv[:, :, 1], EPS_LN, None, ALU.add)\
                            .then_inc(S["veps_made"], 1)
                        wait(pool, "veps_made", n + 1)
                        nc.gpsimd.tensor_tensor(rstd[:, :], veps[:, :], halfs[:, :], ALU.pow)\
                            .then_inc(S["rstd_made"], 1)
                    if scan:
                        gate(pool, k, p, v)
                        if v >= POOL_LAG:
                            c_product(pool, k, p, v - POOL_LAG)
                        elif has_previous(k):
                            c_product(pool, k - 1, r, v + U - POOL_LAG)
                    if dense and v in EARLY:
                        step_size(pool, gd, r, EARLY.index(v))
                    if v in LATE and scan:
                        step_size(pool, k, p, len(EARLY) + LATE.index(v))

            def step_size(pool, g, r, j):
                if j == 0:
                    wait(pool, "soft_ln", g + 1)
                nc.gpsimd.tensor_tensor(delta[:, r, j, :], delta[:, r, j, :], du[:, r, j, :], ALU.add)\
                    .then_inc(S["delta_made"], 1)
                wait(pool, "delta_made", J * g + j + 1)
                nc.gpsimd.tensor_tensor(du[:, r, j, :], delta[:, r, j, :], u[:, r, j, :], ALU.mult)\
                    .then_inc(S["du_made"], 1)

            def gate(pool, k, p, v):
                if v % Q != 3:
                    return
                j = v // Q - 1
                if j < 0:
                    if not has_previous(k):
                        return
                    k, p, j = k - 1, 1 - p, J - 1
                wait(pool, "y_skip", J * k + j + 1)
                nc.gpsimd.tensor_tensor(zs[:, p, j, :], zs[:, p, j, :], yv[:, j % 2, :], ALU.mult)\
                    .then_inc(S["y_gated"], 1)

            def c_product(pool, k, p, v):
                if v == 0:
                    wait(pool, "c_loaded", 16 * k + 16)
                wait(pool, "scanned", U * k + v + 1)
                sl, q = v % SLOTS, v % Q
                nc.gpsimd.tensor_tensor(st[:, sl, :, :], st[:, sl, :, :], bc[:, p, 1, SU * q:SU * q + SU, :],
                                        ALU.mult).then_inc(S["c_times"], 1)

            def tail(pool, k, p):
                for v in range(POOL_LAG):
                    c_product(pool, k - 1, 1 - p, v + U - POOL_LAG)
                gate(pool, k, p, 3)

            walk(pool, body, tail)

        @block.scalar
        def _(act):
            act.wait_ge(S["w_loaded"], 16 * WLOADS)
            nc.scalar.activation(decay[:, :, :], s_alog, ACT.Exp).then_inc(S["decay_exp"], 1)
            act.wait_ge(S["prep_mm"], 1)
            nc.scalar.activation(wj_rep[:, :, :], g0[:, 0:KC * P].rearrange("p (c e) -> p c e", c=KC), ACT.Copy)
            nc.scalar.activation(wi_rep[:, :, :], g0[:, KC * P:2 * KC * P].rearrange("p (c e) -> p c e", c=KC),
                                 ACT.Copy)
            nc.scalar.activation(c0[:, :], g1[:, 0:1], ACT.Copy)
            nc.scalar.activation(bxz[:, :], g1[:, 16:16 + 2 * J], ACT.Copy).then_inc(S["prep_ev"], 1)
            n = 0
            for c in range(KC):
                for e in range(2 * INNER // 512):
                    act.wait_ge(S["prep_mm"], 2 + n)
                    nc.scalar.activation(wxz[:, c, 512 * e:512 * e + 512], (g0, g1)[n % 2][:, :], ACT.Copy)\
                        .then_inc(S["prep_ev"], 1)
                    n += 1
            for j in range(J):
                act.wait_ge(S["prep_mm"], 2 + n)
                nc.scalar.activation(wo[:, j, :], (g0, g1)[n % 2][:, 0:DIM], ACT.Copy).then_inc(S["prep_ev"], 1)
                n += 1

            def decays(act, k, p, v):
                j, q, sl = v // Q, v % Q, v % SLOTS
                if v == 0 and isinstance(k, int) and k == 0:
                    act.wait_ge(S["decay_neg"], 1)
                if q == 0:
                    wait(act, "delta_made", J * k + j + 1)
                wait(act, "scanned", U * k + v + 1 - SLOTS)
                for s in range(SU):
                    a = nc.scalar.activation(
                        dec[:, sl, s, :].rearrange("p (b t) -> p b t", b=PAIR)[:, :, 1:],
                        delta[:, p, j, :].rearrange("p (b t) -> p b t", b=PAIR)[:, :, 1:],
                        ACT.Exp, scale=decay[:, j, SU * q + s:SU * q + s + 1])
                a.then_inc(S["decays"], 1)

            def body(act, k, p, scan, dense, graph):
                r = 1 - p
                if scan:
                    for v in range(ACT_LEAD):
                        decays(act, k, p, v)
                for v in range(U):
                    if scan and v + ACT_LEAD < U:
                        decays(act, k, p, v + ACT_LEAD)
                    if dense:
                        dense_act(act, k + 1, r, v)
                    if graph:
                        graph_act(act, k + 2, p, v)

            def silu_half(act, g, r, h):
                b = slice(4 * h, 4 * h + 4)
                wait(act, "taps", TAPS * (J * g + 4 * h + 4))
                nc.scalar.activation(u[:, r, b, :], u[:, r, b, :], ACT.Silu).then_inc(S["silu_u"], 1)
                wait(act, "z_mm", J * g + 4 * h + 4)
                wait(act, "out_mm", J * (g - 1))
                for j in range(4 * h, 4 * h + 4):
                    a = nc.scalar.activation(zs[:, r, j, :], z_ps[:, j % 4, :], ACT.Silu,
                                             bias=bxz[:, J + j:J + j + 1])
                a.then_inc(S["silu_z"], 1)

            def dense_act(act, g, r, v):
                if v % 2 == 1 and v < 2 * J:
                    j = v // 2
                    wait(act, "u_mm", J // 2 * g + j // 2 + 1)
                    wait(act, "taps", TAPS * (J * g + j - 1))
                    nc.scalar.activation(upad[:, j % 2, :, TAPS - 1:],
                                         u_ps[:, j % 2, :].rearrange("p (b t) -> p b t", b=PAIR),
                                         ACT.Identity, bias=bxz[:, j:j + 1]).then_inc(S["u_biased"], 1)
                if v == 10:
                    silu_half(act, g, r, 0)
                if v == 18:
                    silu_half(act, g, r, 1)
                if v == 20:
                    wait(act, "proj_mm", g + 1)
                    wait(act, "bc_stored", 16 * g)
                    nc.scalar.activation(dbc[:, :], x_ps, ACT.Copy).then_inc(S["dbc_made"], 1)
                if 22 <= v < 22 + J // 2:
                    for j in range(2 * (v - 22), 2 * (v - 22) + 2):
                        wait(act, "dt_mm", J // 2 * g + j // 2 + 1)
                        if j == 0:
                            wait(act, "injected", U * (g - 1))
                        bias = chan[:, TAPS + 1, j:j + 1]
                        nc.scalar.activation(delta[:, r, j, :], d_ps[:, j % 4, :], ACT.Abs, bias=bias)
                        nc.scalar.activation(du[:, r, j, :], d_ps[:, j % 4, :], ACT.Relu, bias=bias)\
                            .then_inc(S["abs_relu"], 1)
                if v == 26:
                    wait(act, "abs_relu", J * g + J)
                    nc.scalar.activation(delta[:, r, :, :], delta[:, r, :, :], ACT.Exp, scale=-1.0)\
                        .then_inc(S["soft_exp"], 1)
                    wait(act, "soft_exp", g + 1)
                    nc.scalar.activation(delta[:, r, :, :], delta[:, r, :, :], ACT.Ln, bias=1.0)\
                        .then_inc(S["soft_ln"], 1)

            def graph_act(act, g, p, v):
                if v == 5:
                    wait(act, "transposed", 2 * g + 1)
                    nc.scalar.activation(xT[:, :, :].rearrange("p c t -> p (c t)"), g0[:, :], ACT.Copy)\
                        .then_inc(S["xT_made"], 1)
                if v == 7:
                    wait(act, "e_mm", g + 1)
                    nc.scalar.activation(att[:, :, :].rearrange("p b i -> p (b i)"), g0[:, 0:PAIR * L],
                                         ACT.Identity, bias=c0[:, 0:1]).then_inc(S["e_biased"], 1)
                if v == 9:
                    wait(act, "e_leaky", g + 1)
                    nc.scalar.activation(att[:, :, :], att[:, :, :], ACT.Exp).then_inc(S["e_exp"], 1)
                if v == 13:
                    wait(act, "rinv_made", g + 1)
                    for b in range(PAIR):
                        a = nc.scalar.activation(x1k[:, b, :], g0[:, b * DIM:(b + 1) * DIM], ACT.Copy,
                                                 scale=rinv[:, b:b + 1])
                    a.then_inc(S["x1k_made"], 1)
                if v == 14:
                    wait(act, "u1T_mm", g + 1)
                    nc.scalar.activation(u1T[:, :, :].rearrange("p c t -> p (c t)"), g1[:, :], ACT.Copy)\
                        .then_inc(S["u1T_made"], 1)
                if v == 16:
                    wait(act, "u2T_mm", g + 1)
                    nc.scalar.activation(u2T.rearrange("p c t -> p (c t)"), g0[:, :], ACT.Copy)\
                        .then_inc(S["u2T_made"], 1)
                if v == 21:
                    wait(act, "h0_mm", g + 1)
                    nc.scalar.activation(x1k[:, :, :].rearrange("p b d -> p (b d)"), g1[:, :], ACT.Copy)\
                        .then_inc(S["h0_made"], 1)
                if v == 29:
                    wait(act, "transposed", 2 * g + 2)
                    wait(act, "z_mm", J * (g - 1))
                    nc.scalar.activation(xnT[:, p, :, :].rearrange("p c t -> p (c t)"), g1[:, :], ACT.Copy)\
                        .then_inc(S["xnT_made"], 1)

            walk(act, body, lambda act, k, p: None)

        @block.tensor
        def _(pe):
            pe.wait_ge(S["w_loaded"], 16 * WLOADS)
            pe.wait_ge(S["reps_made"], 2)
            pe.wait_ge(S["memsets"], 2)
            for half in range(2):
                for c in range(KC):
                    for m in range(KC):
                        nc.tensor.matmul(g0[:, (half * KC + c) * P:(half * KC + c + 1) * P],
                                         s_wvT[:, m, c * P:(c + 1) * P], s_awrep[:, half * KC + m, :],
                                         start=(m == 0), stop=(m == KC - 1))
            for h in range(2 * KC):
                nc.tensor.matmul(g1[:, 0:1], s_bvrep[:, h % KC, :], s_aw[:, h:h + 1],
                                 start=(h == 0), stop=False)
            nc.tensor.matmul(g1[:, 0:1], one1, s_ab[64:65, :], start=False, stop=True)
            for j in range(2 * J):
                for m in range(HC):
                    mm = nc.tensor.matmul(g1[:, 16 + j:17 + j], s_winT[:, m, j * P:(j + 1) * P], s_bfc1[:, m:m + 1],
                                          start=(m == 0), stop=(m == HC - 1))
            mm.then_inc(S["prep_mm"], 1)
            n = 0
            for c in range(KC):
                for e in range(2 * INNER // 512):
                    pe.wait_ge(S["prep_ev"], max(1, n))
                    for m in range(HC):
                        mm = nc.tensor.matmul((g0, g1)[n % 2][:, :], s_fc1[:, m, c * P:(c + 1) * P],
                                              s_winT[:, m, 512 * e:512 * e + 512],
                                              start=(m == 0), stop=(m == HC - 1))
                    mm.then_inc(S["prep_mm"], 1)
                    n += 1
            for j in range(J):
                pe.wait_ge(S["prep_ev"], n)
                for m in range(HC):
                    mm = nc.tensor.matmul((g0, g1)[n % 2][:, 0:DIM], s_wout[:, m, j * P:(j + 1) * P],
                                          s_fc2T[:, m, :], start=(m == 0), stop=(m == HC - 1))
                mm.then_inc(S["prep_mm"], 1)
                n += 1
            pe.wait_ge(S["prep_ev"], n + 1)

            def body(pe, k, p, scan, dense, graph):
                r = 1 - p
                for v in range(U):
                    if dense:
                        dense_pe(pe, k + 1, r, v)
                    if graph:
                        graph_pe(pe, k + 2, p, v)
                    if scan:
                        project_out(pe, k, p, v)
                        if v >= PE_LAG:
                            state_sum(pe, k, p, v - PE_LAG)
                        elif has_previous(k):
                            state_sum(pe, k - 1, r, v + U - PE_LAG)

            def state_sum(pe, k, p, v):
                j, q, sl = v // Q, v % Q, v % SLOTS
                wait(pe, "c_times", U * k + v + 1)
                if q == 0:
                    wait(pe, "y_skip", J * k + j - 1)
                for s in range(SU):
                    mm = nc.tensor.matmul(y_ps[:, j % 2, 0:T], ident[:, :], st[:, sl, s, :],
                                          start=(q == 0 and s == 0), stop=(q == Q - 1 and s == SU - 1))
                mm.then_inc(S["summed"], 1)

            def project_out(pe, k, p, v):
                if v % Q != 1:
                    return
                j = v // Q - 2
                if j < 0:
                    if not has_previous(k):
                        return
                    k, p, j = k - 1, 1 - p, j + J
                if j == 0:
                    wait(pe, "finished", k)
                    nc.tensor.matmul(o_ps[:, :, :].rearrange("p b d -> p (b d)"), one1, bo_row,
                                     start=True, stop=False, skip_group_check=True)
                wait(pe, "y_gated", J * k + j + 1)
                for b in range(PAIR):
                    mm = nc.tensor.matmul(o_ps[:, b, :], zs[:, p, j, b * L:(b + 1) * L], wo[:, j, :],
                                          start=False, stop=(j == J - 1), skip_group_check=True)
                mm.then_inc(S["out_mm"], 1)

            def dense_pe(pe, g, r, v):
                if v % 4 == 0 and v < 2 * J:
                    wait(pe, "xnT_made", g + 1)
                    wait(pe, "u_biased", J * g + v // 2)
                    if v == 0:
                        wait(pe, "dbc_made", g)
                    for j in (v // 2, v // 2 + 1):
                        for c in range(KC):
                            mm = nc.tensor.matmul(u_ps[:, j % 2, :], wxz[:, c, j * P:(j + 1) * P],
                                                  xnT[:, r, c, :], start=(c == 0), stop=(c == KC - 1))
                    mm.then_inc(S["u_mm"], 1)
                if v in Z_STEPS:
                    j = Z_STEPS.index(v)
                    if j == 0:
                        wait(pe, "abs_relu", J * g)
                    wait(pe, "silu_z", 2 * g + j // 4)
                    for c in range(KC):
                        mm = nc.tensor.matmul(z_ps[:, j % 4, :], wxz[:, c, INNER + j * P:INNER + (j + 1) * P],
                                              xnT[:, r, c, :], start=(c == 0), stop=(c == KC - 1))
                    mm.then_inc(S["z_mm"], 1)
                if v in (17, 19):
                    h = int(v == 19)
                    wait(pe, "silu_u", 2 * g + h + 1)
                    if h == 0:
                        wait(pe, "u_biased", J * g + J)
                    for j in range(4 * h, 4 * h + 4):
                        mm = nc.tensor.matmul(x_ps, wx[:, j, :], u[:, r, j, :], start=(j == 0), stop=(j == J - 1))
                    if h == 1:
                        mm.then_inc(S["proj_mm"], 1)
                if 21 <= v < 21 + J // 2:
                    m = v - 21
                    wait(pe, "dbc_made", g + 1)
                    if m == 0:
                        wait(pe, "silu_z", 2 * g + 2)
                    if m >= 2:
                        wait(pe, "abs_relu", J * g + 2 * m - 2)
                    for j in (2 * m, 2 * m + 1):
                        mm = nc.tensor.matmul(d_ps[:, j % 4, :], wdt[:, j * P:(j + 1) * P], dbc[0:RANK, :],
                                              start=True, stop=True)
                    mm.then_inc(S["dt_mm"], 1)

            def graph_pe(pe, g, p, v):
                if v == 4 or v == 28:
                    second = v == 28
                    dst = g1 if second else g0
                    wait(pe, "normed", 2 * g + 1 + second)
                    if second:
                        wait(pe, "h0_made", g + 1)
                    else:
                        wait(pe, "h_summed", g)
                    for c in range(KC):
                        for b in range(PAIR):
                            mm = nc.tensor.transpose(dst[:, c * T + b * L:c * T + (b + 1) * L],
                                                     xn[:, b, c * P:(c + 1) * P], ident[:, :])
                    mm.then_inc(S["transposed"], 1)
                if v == 6:
                    wait(pe, "xT_made", g + 1)
                    for b in range(PAIR):
                        for c in range(KC):
                            cols = xT[:, c, b * L:(b + 1) * L]
                            nc.tensor.matmul(g0[:, b * L:(b + 1) * L], wi_rep[:, c, :], cols,
                                             start=(c == 0), stop=False)
                            mm = nc.tensor.matmul(g0[:, b * L:(b + 1) * L], cols, wj_rep[:, c, :],
                                                  start=False, stop=(c == KC - 1))
                    mm.then_inc(S["e_mm"], 1)
                if v == 11:
                    wait(pe, "alpha_made", g + 1)
                    wait(pe, "xnT_made", g)
                    for b in range(PAIR):
                        nc.tensor.matmul(g0[:, b * DIM:(b + 1) * DIM], att[:, b, :], xn[:, b, :],
                                         start=True, stop=True)
                    for b in range(PAIR):
                        mm = nc.tensor.matmul(g1[:, b:b + 1], att[:, b, :], one_col[:, 0:1], start=True, stop=True)
                    mm.then_inc(S["u1_mm"], 1)
                if v == 13:
                    wait(pe, "rinv_made", g + 1)
                    for c in range(KC):
                        for b in range(PAIR):
                            mm = nc.tensor.matmul(g1[:, c * T + b * L:c * T + (b + 1) * L],
                                                  xn[:, b, c * P:(c + 1) * P], att[:, b, :], start=True, stop=True)
                    mm.then_inc(S["u1T_mm"], 1)
                if v == 15:
                    wait(pe, "x1k_made", g + 1)
                    for c in range(KC):
                        for b in range(PAIR):
                            mm = nc.tensor.matmul(g0[:, c * T + b * L:c * T + (b + 1) * L],
                                                  x1k[:, b, c * P:(c + 1) * P], att[:, b, :], start=True, stop=True)
                    mm.then_inc(S["u2T_mm"], 1)
                if v in (16, 18):
                    b = int(v == 18)
                    if b == 0:
                        wait(pe, "u1T_made", g + 1)
                        nc.tensor.matmul(g1[:, :], ones3, bk_row, start=True, stop=False, skip_group_check=True)
                    for c in range(KC):
                        mm = nc.tensor.matmul(g1[:, b * DIM:(b + 1) * DIM], xT[:, c, b * L:(b + 1) * L],
                                              wks[:, 0, c, :], start=False, stop=(c == KC - 1),
                                              skip_group_check=True)
                    if b == 1:
                        mm.then_inc(S["h0_mm"], 1)
                if v in (18, 20, 22):
                    wait(pe, "u2T_made", g + 1)
                    for b, n in {18: [(0, 0)], 20: [(0, 1), (1, 0)], 22: [(1, 1)]}[v]:
                        for c in range(KC):
                            mm = nc.tensor.matmul(g0[:, b * DIM:(b + 1) * DIM],
                                                  (u1T, u2T)[n][:, c, b * L:(b + 1) * L], wks[:, 1 + n, c, :],
                                                  start=(n == 0 and c == 0), stop=(n == 1 and c == KC - 1))
                    if v == 22:
                        mm.then_inc(S["h_mm"], 1)

            def tail(pe, k, p):
                for v in range(Q + 2):
                    project_out(pe, k, p, v)
                    if v < PE_LAG:
                        state_sum(pe, k - 1, 1 - p, v + U - PE_LAG)

            walk(pe, body, tail)

        @block.vector
        def _(dve):
            nc.vector.memset(one_col[:, :], 1.0)
            nc.vector.memset(ones3, 1.0)
            nc.vector.memset(one1, 1.0)
            nc.vector.memset(halfs[:, :], -0.5).then_inc(S["memsets"], 1)
            nc.vector.memset(dec[:, :, :, :], 0.0)
            nc.vector.memset(upad[:, :, :, :], 0.0).then_inc(S["memsets"], 1)
            dve.wait_ge(S["w_loaded"], 16 * WLOADS)
            nc.vector.tensor_copy(s_awrep, s_aw[:, :, None].to_broadcast([P, 2 * KC, P])).then_inc(S["reps_made"], 1)
            nc.vector.tensor_copy(s_bvrep, s_bv[:, :, None].to_broadcast([P, KC, P])).then_inc(S["reps_made"], 1)
            dve.wait_ge(S["decay_exp"], 1)
            nc.vector.tensor_scalar(decay[:, :, :], decay[:, :, :], -1.0, None, ALU.mult).then_inc(S["decay_neg"], 1)

            def inject(dve, k, p, v):
                j, q, sl = v // Q, v % Q, v % SLOTS
                if v == 0:
                    wait(dve, "b_loaded", 16 * k + 16)
                if q == 0:
                    wait(dve, "du_made", J * k + j + 1)
                wait(dve, "summed", U * k + v + 1 - SLOTS)
                nc.vector.tensor_tensor(st[:, sl, :, :], du[:, p, j, None, :].to_broadcast([P, SU, T]),
                                        bc[:, p, 0, SU * q:SU * q + SU, :], ALU.mult).then_inc(S["injected"], 1)

            def scan_unit(dve, k, p, v):
                sl = v % SLOTS
                wait(dve, "decays", U * k + v + 1)
                wait(dve, "injected", U * k + v + 1)
                flat = st[:, sl, :, :].rearrange("p s t -> p (s t)")
                nc.vector.tensor_tensor_scan(flat, dec[:, sl, :, :].rearrange("p s t -> p (s t)"), flat, 0.0,
                                             ALU.mult, ALU.add).then_inc(S["scanned"], 1)

            def skip_term(dve, k, p, v):
                if v % Q != 2:
                    return
                j = v // Q - 1
                if j < 0:
                    if not has_previous(k):
                        return
                    k, p, j = k - 1, 1 - p, J - 1
                wait(dve, "summed", U * k + Q * (j + 1))
                wait(dve, "y_gated", J * k + j - 1)
                nc.vector.scalar_tensor_tensor(yv[:, j % 2, :], u[:, p, j, :], chan[:, TAPS + 2, j:j + 1],
                                               y_ps[:, j % 2, 0:T], ALU.mult, ALU.add).then_inc(S["y_skip"], 1)

            def finish(dve, k):
                wait(dve, "out_mm", J * k + J)
                wait(dve, "x1_reloaded", 16 * k + 16)
                nc.vector.tensor_tensor(last_x[:, :, :], o_ps[:, :, :], last_x[:, :, :], ALU.add)\
                    .then_inc(S["finished"], 1)

            def tap(dve, g, r, v, second):
                if not 2 <= v < 2 * J + 2:
                    return
                j = v // 2 - 1
                m = 2 * (v % 2) + second
                n = TAPS * (J * g + j) + m
                dst = u[:, r, j, :].rearrange("p (b t) -> p b t", b=PAIR)
                src = upad[:, j % 2, :, m:m + L]
                if m == 0:
                    wait(dve, "u_biased", J * g + j + 1)
                    nc.vector.tensor_scalar(dst, src, chan[:, 0, j:j + 1], chan[:, TAPS, j:j + 1],
                                            ALU.mult, ALU.add).then_inc(S["taps"], 1)
                else:
                    wait(dve, "taps", n)
                    nc.vector.scalar_tensor_tensor(dst, src, chan[:, m, j:j + 1], dst, ALU.mult, ALU.add)\
                        .then_inc(S["taps"], 1)

            def graph_dve(dve, g, v, late):
                if (v, late) in ((1, 0), (25, 0)):
                    second = v == 25
                    if second:
                        wait(dve, "x1_made", g + 1)
                    else:
                        wait(dve, "x_loaded", 16 * g + 16)
                    for b in range(PAIR):
                        a = nc.vector.bn_stats(bstat[:, b, :], xg[:, b, :])
                    a.then_inc(S["stats"], 1)
                if (v, late) in ((1, 1), (25, 1)):
                    second = v == 25
                    wait(dve, "stats", 2 * g + 1 + second)
                    stand(dve)
                    for b in range(PAIR):
                        a = nc.vector.bn_aggr(mv[:, b, :], bstat[:, b, :])
                    a.then_inc(S["aggr"], 1)
                if (v, late) in ((3, 0), (27, 0)):
                    second = v == 27
                    wait(dve, "rstd_made", 2 * g + 1 + second)
                    if second:
                        wait(dve, "h_mm", g + 1)
                    else:
                        wait(dve, "transposed", 2 * g)
                    for b in range(PAIR):
                        a = nc.vector.tensor_scalar(xn[:, b, :], xg[:, b, :], mv[:, b, 0:1], rstd[:, b:b + 1],
                                                    ALU.subtract, ALU.mult)
                    a.then_inc(S["normed"], 1)
                if (v, late) == (8, 0):
                    wait(dve, "e_biased", g + 1)
                    nc.vector.scalar_tensor_tensor(att[:, :, :], att[:, :, :], 0.2, att[:, :, :],
                                                   ALU.mult, ALU.max).then_inc(S["e_leaky"], 1)
                if (v, late) == (10, 0):
                    wait(dve, "e_exp", g + 1)
                    wait(dve, "adj_loaded", 16 * g + 16)
                    nc.vector.tensor_tensor(att[:, :, :], att[:, :, :], adjt[:, :, :], ALU.mult)\
                        .then_inc(S["alpha_made"], 1)
                if (v, late) == (12, 0):
                    wait(dve, "u1_mm", g + 1)
                    nc.vector.tensor_scalar(rowsum[:, :], g1[:, 0:PAIR], EPS_ROW, None, ALU.add)\
                        .then_inc(S["rowsum_eps"], 1)
                    wait(dve, "rowsum_eps", g + 1)
                    nc.vector.reciprocal(rinv[:, :], rowsum[:, :]).then_inc(S["rinv_made"], 1)
                if (v, late) == (24, 0):
                    wait(dve, "h0_made", g + 1)
                    wait(dve, "h_mm", g + 1)
                    for b in range(PAIR):
                        a = nc.vector.scalar_tensor_tensor(x1k[:, b, :], g0[:, b * DIM:(b + 1) * DIM],
                                                           rinv[:, b:b + 1], x1k[:, b, :], ALU.mult, ALU.add)
                    a.then_inc(S["h_summed"], 1)
                if (v, late) == (24, 1):
                    wait(dve, "h_summed", g + 1)
                    nc.vector.scalar_tensor_tensor(xg[:, :, :], x1k[:, :, :], 0.0, xg[:, :, :],
                                                   ALU.max, ALU.add).then_inc(S["x1_made"], 1)

            def body(dve, k, p, scan, dense, graph):
                r = 1 - p
                if scan:
                    inject(dve, k, p, 0)
                for v in range(U):
                    if dense:
                        tap(dve, k + 1, r, v, 0)
                    if scan and v + 1 < U:
                        inject(dve, k, p, v + 1)
                    if dense:
                        tap(dve, k + 1, r, v, 1)
                    if graph:
                        graph_dve(dve, k + 2, v, 0)
                    if scan:
                        scan_unit(dve, k, p, v)
                        skip_term(dve, k, p, v)
                        if v == 7 and has_previous(k):
                            finish(dve, k - 1)
                    if graph:
                        graph_dve(dve, k + 2, v, 1)

            def tail(dve, k, p):
                skip_term(dve, k, p, 2)
                finish(dve, k - 1)

            walk(dve, body, tail)


def kernel(**inputs):
    import numpy as np
    import concourse.bacc as bacc
    from concourse.bass_utils import run_bass_kernel_spmd

    a = {n: np.asarray(v) for n, v in inputs.items()}

    def chunks(w):
        return w.reshape(w.shape[0] // P, P, *w.shape[1:]).swapaxes(0, 1)

    g, f = "L0_gnn_", "L0_ffn_"
    ins = {
        "x": a["x"], "adjT": a["adj"].swapaxes(1, 2),
        "w_inT": chunks(a[f + "W_in"].T), "w_fc1": chunks(a[f + "W_fc1"]),
        "w_out": chunks(a[f + "W_out"]), "w_fc2T": chunks(a[f + "W_fc2"].T),
        "w_vT": chunks(a[g + "Wv"].T), "aw": chunks(a[g + "aw"][:, 0]), "bv": chunks(a[g + "bv"]),
        "ab": a[g + "ab"].reshape(1, 1), "wk": a[g + "Wk"].reshape(HOPS, KC, P, DIM).transpose(2, 0, 1, 3),
        "bk": a[g + "bk"], "b_fc1": chunks(a[f + "b_fc1"]),
        "conv_w": chunks(a[f + "conv_w"]).swapaxes(1, 2), "conv_b": chunks(a[f + "conv_b"]),
        "w_xT": chunks(a[f + "W_xproj"].T), "w_dtT": a[f + "W_dt"].T, "b_dt": chunks(a[f + "b_dt"]),
        "a_log": chunks(a[f + "A_log"]), "skip": chunks(a[f + "D"]), "b_fc2": a[f + "b_fc2"].reshape(1, DIM),
        "ident_in": np.eye(P, dtype=np.float32),
    }
    nc = bacc.Bacc("TRN2", target_bir_lowering=False, num_devices=1, dynamic_dma_scratch_size=1024)
    arrays, args = {}, {}
    for name, v in ins.items():
        v = np.ascontiguousarray(v)
        arrays[name + "_dram"] = v
        args[name] = nc.dram_tensor(name + "_dram", v.shape, mybir.dt.from_np(v.dtype), kind="ExternalInput").ap()
    out = nc.dram_tensor("out_dram", (BATCH, L, DIM), F32, kind="ExternalOutput").ap()
    build(nc, **args, out=out)
    r = run_bass_kernel_spmd(nc, [arrays], core_ids=[0])
    return r.results[0]["out_dram"]
```

```python
from contextlib import ExitStack

import concourse.bass as bass
from concourse import mybir

F32 = mybir.dt.float32
ALU = mybir.AluOpType
ACT = mybir.ActivationFunctionType

BATCH, L, DIM = 64, 128, 256
P = 128
INNER = 1024
STATE = 16
RANK = 32
TAPS = 4
HID = 512
HOPS = 3
PAIR = 2
GROUPS = BATCH // PAIR
T = PAIR * L
KC = DIM // P
HC = HID // P
J = INNER // P
PROJ = RANK + 2 * STATE
SU = 4
Q = STATE // SU
U = J * Q
SLOTS = 4
EPS_LN = 1e-5
EPS_ROW = 1e-12
EARLY = (27, 29)
LATE = (2, 5, 9, 13, 17, 21)
TURN = 10
Z_STEPS = (2, 3, 5, 7, 11, 13, 14, 15)
ACT_LEAD, POOL_LAG, PE_LAG = 2, 0, 1


def build(nc, x, adjT, w_inT, w_fc1, w_out, w_fc2T, w_vT, aw, bv, ab, wk, bk, b_fc1, conv_w, conv_b,
          w_xT, w_dtT, b_dt, a_log, skip, b_fc2, ident_in, out):
    bc_dram = nc.dram_tensor("bc_dram", [2, 2, STATE * T], F32).ap()
    x1_dram = nc.dram_tensor("x1_dram", [GROUPS, P, PAIR * DIM], F32).ap()

    with ExitStack() as ctx:
        def sb(name, shape):
            return ctx.enter_context(nc.sbuf_tensor(name, shape, F32))

        def sem(name):
            return ctx.enter_context(nc.semaphore(name))

        wxz = sb("wxz", [P, KC, 2 * INNER])
        wo = sb("wo", [P, J, DIM])
        wx = sb("wx", [P, J, PROJ])
        rows = sb("rows", [P, INNER])
        wks = sb("wks", [P, HOPS, KC, DIM])
        wi_rep = sb("wi_rep", [P, KC, P])
        wj_rep = sb("wj_rep", [P, KC, P])
        ident = sb("ident", [P, P])
        decay = sb("decay", [P, J, STATE])
        bxz = sb("bxz", [P, 2 * J])
        chan = sb("chan", [P, TAPS + 3, J])
        bconv = sb("bconv", [P, J])
        c0 = sb("c0", [P, 1])
        one_col = sb("one_col", [P, 1])
        halfs = sb("halfs", [P, PAIR])
        ones3 = rows[32:32 + HOPS, PAIR * DIM:PAIR * DIM + P]
        one1 = rows[64:65, PAIR * DIM:PAIR * DIM + P]
        wdt = rows[0:RANK, :]
        bk_row = rows[32:32 + HOPS, 0:PAIR * DIM]
        bo_row = rows[64:65, 0:PAIR * DIM]

        bc = sb("bc", [P, 2, 2, STATE, T])
        delta = sb("delta", [P, 2, J, T])
        du = sb("du", [P, 2, J, T])
        u = sb("u", [P, 2, J, T])
        zs = sb("zs", [P, 2, J, T])
        xnT = sb("xnT", [P, 2, KC, T])

        dec = sb("dec", [P, SLOTS, SU, T])
        st = sb("st", [P, SLOTS, SU, T])
        upad = sb("upad", [P, 2, PAIR, L + TAPS - 1])
        yv = sb("yv", [P, 2, T])
        dbc = sb("dbc", [PROJ, T])

        xg = sb("xg", [P, PAIR, DIM])
        adjt = sb("adjt", [P, PAIR, L])
        xn = sb("xn", [P, PAIR, DIM])
        xT = sb("xT", [P, KC, T])
        att = sb("att", [P, PAIR, L])
        x1k = sb("x1k", [P, PAIR, DIM])
        u1T = sb("u1T", [P, KC, T])
        u2T = xn[:, :, :].rearrange("p b d -> p (b d)").rearrange("p (c t) -> p c t", c=KC)
        last_x = sb("last_x", [P, PAIR, DIM])
        bstat = sb("bstat", [P, PAIR, 6])
        mv = sb("mv", [P, PAIR, 2])
        veps = sb("veps", [P, PAIR])
        rstd = sb("rstd", [P, PAIR])
        rowsum = sb("rowsum", [P, PAIR])
        rinv = sb("rinv", [P, PAIR])

        def bank(name, shape):
            return ctx.enter_context(nc.psum_tensor(name, shape, F32))

        y_ps = bank("y_ps", [P, 2, 512])
        u_ps = bank("u_ps", [P, 2, T])
        z_ps = bank("z_ps", [P, 4, T])
        o_ps = bank("o_ps", [P, PAIR, DIM])
        g0 = bank("g0", [P, 512])
        g1 = bank("g1", [P, 512])
        x_ps = u_ps[0:PROJ, 0, :]
        d_ps = z_ps

        stage = bc[:, :, :, :, :].rearrange("p a b s t -> p (a b s t)")
        at = [0]

        def staged(*dims):
            n = 1
            for d in dims:
                n *= d
            v = stage[:, at[0]:at[0] + n]
            at[0] += n
            return v

        s_winT = staged(HC, 2 * INNER).rearrange("p (c e) -> p c e", c=HC)
        s_fc1 = staged(HC, DIM).rearrange("p (c e) -> p c e", c=HC)
        s_wout = staged(HC, INNER).rearrange("p (c e) -> p c e", c=HC)
        s_fc2T = staged(HC, DIM).rearrange("p (c e) -> p c e", c=HC)
        s_wvT = staged(KC, DIM).rearrange("p (c e) -> p c e", c=KC)
        s_awrep = staged(2 * KC, P).rearrange("p (c e) -> p c e", c=2 * KC)
        s_aw = staged(2 * KC)
        s_bv = staged(KC)
        s_bvrep = staged(KC, P).rearrange("p (c e) -> p c e", c=KC)
        s_bfc1 = staged(HC)
        s_ab = staged(1)
        s_alog = staged(J * STATE).rearrange("p (j s) -> p j s", j=J)

        names = """stands w_graph w_dense memsets reps_made attn_mm attn_made fold_mm folded bconv_made decay_exp decay_neg
        x_loaded adj_loaded stats aggr veps_made rstd_made normed transposed xT_made xnT_made
        e_mm e_biased e_leaky e_exp alpha_made u1_mm rowsum_eps rinv_made x1k_made u1T_mm u1T_made u2T_mm u2T_made
        h0_mm h_mm h0_made h_summed x1_made x1_stored x1_reloaded
        u_mm z_mm u_biased taps silu_u silu_z proj_mm dbc_made bc_stored b_loaded c_loaded
        dt_mm abs_relu soft_exp soft_ln delta_made du_made
        decays injected scanned c_times summed y_skip y_gated out_mm finished out_stored"""
        S = {n: sem(n) for n in names.split()}

        def wait(eng, name, value):
            if isinstance(value, int) and value <= 0:
                return
            eng.wait_ge(S[name], value)

        def stand(eng):
            eng.sem_inc(S["stands"], 1)

        def walk(eng, body, tail):
            body(eng, -3, 1, False, False, False, True)
            body(eng, -2, 0, False, False, True, True)
            body(eng, -1, 1, False, True, True, True)
            body(eng, 0, 0, True, True, True, True)
            with eng.Fori(0, (GROUPS - 4) // 2) as i:
                body(eng, i * 2 + 1, 1, True, True, True, True)
                body(eng, i * 2 + 2, 0, True, True, True, True)
            body(eng, GROUPS - 3, 1, True, True, True, False)
            body(eng, GROUPS - 2, 0, True, True, False, False)
            body(eng, GROUPS - 1, 1, True, False, False, False)
            tail(eng, GROUPS, 0)

        def graph_step(k, p, v, ends, begins):
            if v < TURN:
                return (k + 2, p, v + U - TURN) if ends else None
            return (k + 3, 1 - p, v - TURN) if begins else None

        def has_previous(k):
            return not (isinstance(k, int) and k <= 0)

        block = ctx.enter_context(nc.Block())

        GRAPH_LOADS = [
            (s_wvT, w_vT), (s_aw, aw), (s_bv, bv), (s_ab[64:65, :], ab), (ident[:, :], ident_in),
            (wks[:, :, :, :], wk), (rows[32:32 + HOPS, 0:DIM], bk), (rows[32:32 + HOPS, DIM:2 * DIM], bk),
        ]
        DENSE_LOADS = [
            (s_fc1, w_fc1), (s_winT, w_inT), (s_bfc1, b_fc1), (s_alog, a_log),
            (chan[:, 0:TAPS, :], conv_w), (chan[:, TAPS, :], conv_b), (chan[:, TAPS + 1, :], b_dt),
            (chan[:, TAPS + 2, :], skip), (wx[:, :, :], w_xT), (wdt, w_dtT), (s_wout, w_out), (s_fc2T, w_fc2T),
            (rows[64:65, 0:DIM], b_fc2), (rows[64:65, DIM:2 * DIM], b_fc2),
        ]
        FOLDS = KC * (2 * INNER // 512)

        @block.sync
        def _(sp):
            for dst, src in GRAPH_LOADS:
                sp.dma_start(dst, src).then_inc(S["w_graph"], 16)

            def body(sp, k, p, scan, dense, ends, begins):
                if ends:
                    g = k + 2
                    wait(sp, "x1_made", g + 1)
                    stand(sp)
                    sp.dma_start(x1_dram[bass.ds(g, 1)].rearrange("a p n -> (a p) n")
                                 if not isinstance(g, int) else x1_dram[g],
                                 xg[:, :, :].rearrange("p b d -> p (b d)")).then_inc(S["x1_stored"], 16)
                g = k + 3
                if begins:
                    wait(sp, "x1_stored", 16 * g)
                    stand(sp)
                    wait(sp, "normed", 2 * g)
                    stand(sp)
                    sp.dma_start(xg[:, :, :], x[bass.ds(g * PAIR, PAIR)].rearrange("b t d -> t b d")
                                 if not isinstance(g, int) else
                                 x[g * PAIR:(g + 1) * PAIR].rearrange("b t d -> t b d")).then_inc(S["x_loaded"], 16)
                    wait(sp, "alpha_made", g)
                    stand(sp)
                    sp.dma_start(adjt[:, :, :], adjT[bass.ds(g * PAIR, PAIR)].rearrange("b j i -> j b i")
                                 if not isinstance(g, int) else
                                 adjT[g * PAIR:(g + 1) * PAIR].rearrange("b j i -> j b i")).then_inc(S["adj_loaded"], 16)
                if has_previous(k) and scan:
                    store_out(sp, k - 1)
                if scan:
                    wait(sp, "out_stored", 16 * k)
                    stand(sp)
                    sp.dma_start(last_x[:, :, :].rearrange("p b d -> p (b d)"),
                                 x1_dram[bass.ds(k, 1)].rearrange("a p n -> (a p) n")
                                 if not isinstance(k, int) else x1_dram[k]).then_inc(S["x1_reloaded"], 16)
                if dense:
                    g = k + 1
                    r = 1 - p
                    wait(sp, "dbc_made", g + 1)
                    stand(sp)
                    wait(sp, "b_loaded", 16 * g)
                    stand(sp)
                    sp.dma_start(bc_dram[r].rearrange("a (s t) -> (a s) t", s=STATE),
                                 dbc[RANK:PROJ, :]).then_inc(S["bc_stored"], 16)
                    wait(sp, "bc_stored", 16 * g + 16)
                    stand(sp)
                    wait(sp, "injected", U * (g - 1))
                    stand(sp)
                    sp.dma_start(bc[:, r, 0, :, :].rearrange("p s t -> p (s t)"),
                                 bc_dram[r, 0:1].to_broadcast([P, STATE * T])).then_inc(S["b_loaded"], 16)
                    wait(sp, "c_times", U * (g - 1))
                    stand(sp)
                    sp.dma_start(bc[:, r, 1, :, :].rearrange("p s t -> p (s t)"),
                                 bc_dram[r, 1:2].to_broadcast([P, STATE * T])).then_inc(S["c_loaded"], 16)

            def store_out(sp, g):
                wait(sp, "finished", g + 1)
                stand(sp)
                sp.dma_start(out[bass.ds(g * PAIR, PAIR)].rearrange("b t d -> t b d")
                             if not isinstance(g, int) else
                             out[g * PAIR:(g + 1) * PAIR].rearrange("b t d -> t b d"),
                             last_x[:, :, :]).then_inc(S["out_stored"], 16)

            def tail(sp, k, p):
                store_out(sp, k - 1)
                sp.wait_ge(S["out_stored"], 16 * GROUPS)
                sp.wait_ge(S["x1_stored"], 16 * GROUPS)
                sp.wait_ge(S["bc_stored"], 16 * GROUPS)

            walk(sp, body, tail)

        @block.gpsimd
        def _(pool):
            def body(pool, k, p, scan, dense, ends, begins):
                r = 1 - p
                gd = k + 1
                for v in range(U):
                    gs = graph_step(k, p, v, ends, begins)
                    if gs and gs[2] in (2, 26):
                        n = 2 * gs[0] + (gs[2] == 26)
                        wait(pool, "aggr", n + 1)
                        stand(pool)
                        nc.gpsimd.tensor_scalar(veps[:, :], mv[:, :, 1], EPS_LN, None, ALU.add)\
                            .then_inc(S["veps_made"], 1)
                        wait(pool, "veps_made", n + 1)
                        nc.gpsimd.tensor_tensor(rstd[:, :], veps[:, :], halfs[:, :], ALU.pow)\
                            .then_inc(S["rstd_made"], 1)
                    if scan:
                        gate(pool, k, p, v)
                        if v >= POOL_LAG:
                            c_product(pool, k, p, v - POOL_LAG)
                        elif has_previous(k):
                            c_product(pool, k - 1, r, v + U - POOL_LAG)
                    if dense and v in EARLY:
                        step_size(pool, gd, r, EARLY.index(v))
                    if v in LATE and scan:
                        step_size(pool, k, p, len(EARLY) + LATE.index(v))

            def step_size(pool, g, r, j):
                if j == 0:
                    wait(pool, "soft_ln", g + 1)
                nc.gpsimd.tensor_tensor(delta[:, r, j, :], delta[:, r, j, :], du[:, r, j, :], ALU.add)\
                    .then_inc(S["delta_made"], 1)
                wait(pool, "delta_made", J * g + j + 1)
                nc.gpsimd.tensor_tensor(du[:, r, j, :], delta[:, r, j, :], u[:, r, j, :], ALU.mult)\
                    .then_inc(S["du_made"], 1)

            def gate(pool, k, p, v):
                if v % Q != 3:
                    return
                j = v // Q - 1
                if j < 0:
                    if not has_previous(k):
                        return
                    k, p, j = k - 1, 1 - p, J - 1
                wait(pool, "y_skip", J * k + j + 1)
                nc.gpsimd.tensor_tensor(zs[:, p, j, :], zs[:, p, j, :], yv[:, j % 2, :], ALU.mult)\
                    .then_inc(S["y_gated"], 1)

            def c_product(pool, k, p, v):
                if v == 0:
                    wait(pool, "c_loaded", 16 * k + 16)
                wait(pool, "scanned", U * k + v + 1)
                sl, q = v % SLOTS, v % Q
                nc.gpsimd.tensor_tensor(st[:, sl, :, :], st[:, sl, :, :], bc[:, p, 1, SU * q:SU * q + SU, :],
                                        ALU.mult).then_inc(S["c_times"], 1)

            def tail(pool, k, p):
                for v in range(POOL_LAG):
                    c_product(pool, k - 1, 1 - p, v + U - POOL_LAG)
                gate(pool, k, p, 3)

            walk(pool, body, tail)

        @block.scalar
        def _(act):
            for dst, src in DENSE_LOADS:
                act.dma_start(dst, src).then_inc(S["w_dense"], 16)
            act.wait_ge(S["attn_mm"], 1)
            nc.scalar.activation(wj_rep[:, :, :], g0[:, 0:KC * P].rearrange("p (c e) -> p c e", c=KC), ACT.Copy)
            nc.scalar.activation(wi_rep[:, :, :], g0[:, KC * P:2 * KC * P].rearrange("p (c e) -> p c e", c=KC),
                                 ACT.Copy)
            nc.scalar.activation(c0[:, :], g1[:, 0:1], ACT.Copy).then_inc(S["attn_made"], 1)

            def fold_out(act, v, first):
                if v == TURN and first:
                    act.wait_ge(S["w_dense"], 16 * len(DENSE_LOADS))
                    nc.scalar.activation(decay[:, :, :], s_alog, ACT.Exp).then_inc(S["decay_exp"], 1)
                if v == U - 1 and first:
                    act.wait_ge(S["fold_mm"], FOLDS + 1)
                    nc.scalar.activation(bxz[:, :], y_ps[:, 0, 0:2 * J], ACT.Copy).then_inc(S["folded"], 1)
                n = v - TURN if first else FOLDS + v
                if not (0 <= n < FOLDS if first else n < FOLDS + J):
                    return
                act.wait_ge(S["fold_mm"], n + 1 if first else n + 2)
                if n < FOLDS:
                    c, e = n // (FOLDS // KC), n % (FOLDS // KC)
                    a = nc.scalar.activation(wxz[:, c, 512 * e:512 * e + 512], y_ps[:, n % 2, :], ACT.Copy)
                else:
                    a = nc.scalar.activation(wo[:, n - FOLDS, :], y_ps[:, n % 2, 0:DIM], ACT.Copy)
                a.then_inc(S["folded"], 1)

            def decays(act, k, p, v):
                j, q, sl = v // Q, v % Q, v % SLOTS
                if v == 0 and isinstance(k, int) and k == 0:
                    act.wait_ge(S["decay_neg"], 1)
                if q == 0:
                    wait(act, "delta_made", J * k + j + 1)
                wait(act, "scanned", U * k + v + 1 - SLOTS)
                for s in range(SU):
                    a = nc.scalar.activation(
                        dec[:, sl, s, :].rearrange("p (b t) -> p b t", b=PAIR)[:, :, 1:],
                        delta[:, p, j, :].rearrange("p (b t) -> p b t", b=PAIR)[:, :, 1:],
                        ACT.Exp, scale=decay[:, j, SU * q + s:SU * q + s + 1])
                a.then_inc(S["decays"], 1)

            def body(act, k, p, scan, dense, ends, begins):
                r = 1 - p
                if scan:
                    for v in range(ACT_LEAD):
                        decays(act, k, p, v)
                for v in range(U):
                    if scan and v + ACT_LEAD < U:
                        decays(act, k, p, v + ACT_LEAD)
                    if dense:
                        dense_act(act, k + 1, r, v)
                    if not scan and not dense:
                        fold_out(act, v, not ends)
                    gs = graph_step(k, p, v, ends, begins)
                    if gs:
                        graph_act(act, *gs)

            def silu_half(act, g, r, h):
                b = slice(4 * h, 4 * h + 4)
                wait(act, "taps", (TAPS - 1) * (J * g + 4 * h + 4))
                nc.scalar.activation(u[:, r, b, :], u[:, r, b, :], ACT.Silu).then_inc(S["silu_u"], 1)
                wait(act, "z_mm", J * g + 4 * h + 4)
                wait(act, "out_mm", J * (g - 1))
                for j in range(4 * h, 4 * h + 4):
                    a = nc.scalar.activation(zs[:, r, j, :], z_ps[:, j % 4, :], ACT.Silu,
                                             bias=bxz[:, J + j:J + j + 1])
                a.then_inc(S["silu_z"], 1)

            def dense_act(act, g, r, v):
                if v % 2 == 1 and v < 2 * J:
                    j = v // 2
                    wait(act, "u_mm", J // 2 * g + j // 2 + 1)
                    wait(act, "taps", (TAPS - 1) * (J * g + j - 1))
                    nc.scalar.activation(upad[:, j % 2, :, TAPS - 1:],
                                         u_ps[:, j % 2, :].rearrange("p (b t) -> p b t", b=PAIR),
                                         ACT.Identity, bias=bxz[:, j:j + 1])
                    wait(act, "y_skip", J * (g - 2) + j + 1)
                    if isinstance(g, int) and g == 0 and j == 0:
                        act.wait_ge(S["bconv_made"], 2)
                    nc.scalar.activation(u[:, r, j, :], u_ps[:, j % 2, :], ACT.Identity, bias=bconv[:, j:j + 1],
                                         scale=chan[:, TAPS - 1, j:j + 1]).then_inc(S["u_biased"], 1)
                if v == 10:
                    silu_half(act, g, r, 0)
                if v == 18:
                    silu_half(act, g, r, 1)
                if v == 20:
                    wait(act, "proj_mm", g + 1)
                    wait(act, "bc_stored", 16 * g)
                    nc.scalar.activation(dbc[:, :], x_ps, ACT.Copy).then_inc(S["dbc_made"], 1)
                if 22 <= v < 22 + J // 2:
                    for j in range(2 * (v - 22), 2 * (v - 22) + 2):
                        wait(act, "dt_mm", J // 2 * g + j // 2 + 1)
                        if j == 0:
                            wait(act, "injected", U * (g - 1))
                        bias = chan[:, TAPS + 1, j:j + 1]
                        nc.scalar.activation(delta[:, r, j, :], d_ps[:, j % 4, :], ACT.Abs, bias=bias)
                        nc.scalar.activation(du[:, r, j, :], d_ps[:, j % 4, :], ACT.Relu, bias=bias)\
                            .then_inc(S["abs_relu"], 1)
                if v == 26:
                    wait(act, "abs_relu", J * g + J)
                    nc.scalar.activation(delta[:, r, :, :], delta[:, r, :, :], ACT.Exp, scale=-1.0)\
                        .then_inc(S["soft_exp"], 1)
                    wait(act, "soft_exp", g + 1)
                    nc.scalar.activation(delta[:, r, :, :], delta[:, r, :, :], ACT.Ln, bias=1.0)\
                        .then_inc(S["soft_ln"], 1)

            def graph_act(act, g, p, v):
                if v == 5:
                    wait(act, "transposed", 2 * g + 1)
                    nc.scalar.activation(xT[:, :, :].rearrange("p c t -> p (c t)"), g0[:, :], ACT.Copy)\
                        .then_inc(S["xT_made"], 1)
                if v == 7:
                    wait(act, "e_mm", g + 1)
                    nc.scalar.activation(att[:, :, :].rearrange("p b i -> p (b i)"), g0[:, 0:PAIR * L],
                                         ACT.Identity, bias=c0[:, 0:1]).then_inc(S["e_biased"], 1)
                if v == 9:
                    wait(act, "e_leaky", g + 1)
                    nc.scalar.activation(att[:, :, :], att[:, :, :], ACT.Exp).then_inc(S["e_exp"], 1)
                if v == 13:
                    wait(act, "rinv_made", g + 1)
                    for b in range(PAIR):
                        a = nc.scalar.activation(x1k[:, b, :], g0[:, b * DIM:(b + 1) * DIM], ACT.Copy,
                                                 scale=rinv[:, b:b + 1])
                    a.then_inc(S["x1k_made"], 1)
                if v == 14:
                    wait(act, "u1T_mm", g + 1)
                    nc.scalar.activation(u1T[:, :, :].rearrange("p c t -> p (c t)"), g1[:, :], ACT.Copy)\
                        .then_inc(S["u1T_made"], 1)
                if v == 16:
                    wait(act, "u2T_mm", g + 1)
                    nc.scalar.activation(u2T.rearrange("p c t -> p (c t)"), g0[:, :], ACT.Copy)\
                        .then_inc(S["u2T_made"], 1)
                if v == 21:
                    wait(act, "h0_mm", g + 1)
                    nc.scalar.activation(x1k[:, :, :].rearrange("p b d -> p (b d)"), g1[:, :], ACT.Copy)\
                        .then_inc(S["h0_made"], 1)
                if v == 29:
                    wait(act, "transposed", 2 * g + 2)
                    wait(act, "z_mm", J * (g - 1))
                    nc.scalar.activation(xnT[:, p, :, :].rearrange("p c t -> p (c t)"), g1[:, :], ACT.Copy)\
                        .then_inc(S["xnT_made"], 1)

            walk(act, body, lambda act, k, p: None)

        @block.tensor
        def _(pe):
            pe.wait_ge(S["w_graph"], 16 * len(GRAPH_LOADS))
            pe.wait_ge(S["reps_made"], 2)
            pe.wait_ge(S["memsets"], 2)
            for half in range(2):
                for c in range(KC):
                    for m in range(KC):
                        nc.tensor.matmul(g0[:, (half * KC + c) * P:(half * KC + c + 1) * P],
                                         s_wvT[:, m, c * P:(c + 1) * P], s_awrep[:, half * KC + m, :],
                                         start=(m == 0), stop=(m == KC - 1))
            for h in range(2 * KC):
                nc.tensor.matmul(g1[:, 0:1], s_bvrep[:, h % KC, :], s_aw[:, h:h + 1],
                                 start=(h == 0), stop=False)
            nc.tensor.matmul(g1[:, 0:1], one1, s_ab[64:65, :], start=False, stop=True).then_inc(S["attn_mm"], 1)
            pe.wait_ge(S["attn_made"], 1)

            def fold(pe, v, first):
                if v == U - 1 and first:
                    pe.wait_ge(S["folded"], FOLDS)
                    for j in range(2 * J):
                        for m in range(HC):
                            mm = nc.tensor.matmul(y_ps[:, 0, j:j + 1], s_winT[:, m, j * P:(j + 1) * P],
                                                  s_bfc1[:, m:m + 1], start=(m == 0), stop=(m == HC - 1))
                    mm.then_inc(S["fold_mm"], 1)
                n = v - TURN if first else FOLDS + v
                if not (0 <= n < FOLDS if first else n < FOLDS + J):
                    return
                if n == 0:
                    pe.wait_ge(S["w_dense"], 16 * len(DENSE_LOADS))
                wait(pe, "folded", n - 1 if first else max(n, FOLDS + 1))
                for m in range(HC):
                    if n < FOLDS:
                        c, e = n // (FOLDS // KC), n % (FOLDS // KC)
                        mm = nc.tensor.matmul(y_ps[:, n % 2, :], s_fc1[:, m, c * P:(c + 1) * P],
                                              s_winT[:, m, 512 * e:512 * e + 512],
                                              start=(m == 0), stop=(m == HC - 1))
                    else:
                        j = n - FOLDS
                        mm = nc.tensor.matmul(y_ps[:, n % 2, 0:DIM], s_wout[:, m, j * P:(j + 1) * P],
                                              s_fc2T[:, m, :], start=(m == 0), stop=(m == HC - 1))
                mm.then_inc(S["fold_mm"], 1)

            def body(pe, k, p, scan, dense, ends, begins):
                r = 1 - p
                for v in range(U):
                    if dense:
                        dense_pe(pe, k + 1, r, v)
                    if not scan and not dense:
                        fold(pe, v, not ends)
                    gs = graph_step(k, p, v, ends, begins)
                    if gs:
                        graph_pe(pe, *gs)
                    if scan:
                        project_out(pe, k, p, v)
                        if v >= PE_LAG:
                            state_sum(pe, k, p, v - PE_LAG)
                        elif has_previous(k):
                            state_sum(pe, k - 1, r, v + U - PE_LAG)

            def state_sum(pe, k, p, v):
                j, q, sl = v // Q, v % Q, v % SLOTS
                wait(pe, "c_times", U * k + v + 1)
                if q == 0:
                    wait(pe, "y_skip", J * k + j - 1)
                    if isinstance(k, int) and k == 0 and j == 0:
                        pe.wait_ge(S["folded"], 1 + FOLDS + J)
                for s in range(SU):
                    mm = nc.tensor.matmul(y_ps[:, j % 2, 0:T], ident[:, :], st[:, sl, s, :],
                                          start=(q == 0 and s == 0), stop=(q == Q - 1 and s == SU - 1))
                mm.then_inc(S["summed"], 1)

            def project_out(pe, k, p, v):
                if v % Q != 1:
                    return
                j = v // Q - 2
                if j < 0:
                    if not has_previous(k):
                        return
                    k, p, j = k - 1, 1 - p, j + J
                if j == 0:
                    wait(pe, "finished", k)
                    nc.tensor.matmul(o_ps[:, :, :].rearrange("p b d -> p (b d)"), one1, bo_row,
                                     start=True, stop=False, skip_group_check=True)
                wait(pe, "y_gated", J * k + j + 1)
                for b in range(PAIR):
                    mm = nc.tensor.matmul(o_ps[:, b, :], zs[:, p, j, b * L:(b + 1) * L], wo[:, j, :],
                                          start=False, stop=(j == J - 1), skip_group_check=True)
                mm.then_inc(S["out_mm"], 1)

            def dense_pe(pe, g, r, v):
                if v % 4 == 0 and v < 2 * J:
                    wait(pe, "xnT_made", g + 1)
                    wait(pe, "u_biased", J * g + v // 2)
                    if v == 0:
                        wait(pe, "dbc_made", g)
                        if isinstance(g, int) and g == 0:
                            pe.wait_ge(S["folded"], 1 + FOLDS)
                    for j in (v // 2, v // 2 + 1):
                        for c in range(KC):
                            mm = nc.tensor.matmul(u_ps[:, j % 2, :], wxz[:, c, j * P:(j + 1) * P],
                                                  xnT[:, r, c, :], start=(c == 0), stop=(c == KC - 1))
                    mm.then_inc(S["u_mm"], 1)
                if v in Z_STEPS:
                    j = Z_STEPS.index(v)
                    if j == 0:
                        wait(pe, "abs_relu", J * g)
                    wait(pe, "silu_z", 2 * g + j // 4)
                    for c in range(KC):
                        mm = nc.tensor.matmul(z_ps[:, j % 4, :], wxz[:, c, INNER + j * P:INNER + (j + 1) * P],
                                              xnT[:, r, c, :], start=(c == 0), stop=(c == KC - 1))
                    mm.then_inc(S["z_mm"], 1)
                if v in (17, 19):
                    h = int(v == 19)
                    wait(pe, "silu_u", 2 * g + h + 1)
                    if h == 0:
                        wait(pe, "u_biased", J * g + J)
                    for j in range(4 * h, 4 * h + 4):
                        mm = nc.tensor.matmul(x_ps, wx[:, j, :], u[:, r, j, :], start=(j == 0), stop=(j == J - 1))
                    if h == 1:
                        mm.then_inc(S["proj_mm"], 1)
                if 21 <= v < 21 + J // 2:
                    m = v - 21
                    wait(pe, "dbc_made", g + 1)
                    if m == 0:
                        wait(pe, "silu_z", 2 * g + 2)
                    if m >= 2:
                        wait(pe, "abs_relu", J * g + 2 * m - 2)
                    for j in (2 * m, 2 * m + 1):
                        mm = nc.tensor.matmul(d_ps[:, j % 4, :], wdt[:, j * P:(j + 1) * P], dbc[0:RANK, :],
                                              start=True, stop=True)
                    mm.then_inc(S["dt_mm"], 1)

            def graph_pe(pe, g, p, v):
                if v == 4 or v == 28:
                    second = v == 28
                    dst = g1 if second else g0
                    wait(pe, "normed", 2 * g + 1 + second)
                    if second:
                        wait(pe, "h0_made", g + 1)
                    else:
                        wait(pe, "h_summed", g)
                    for c in range(KC):
                        for b in range(PAIR):
                            mm = nc.tensor.transpose(dst[:, c * T + b * L:c * T + (b + 1) * L],
                                                     xn[:, b, c * P:(c + 1) * P], ident[:, :])
                    mm.then_inc(S["transposed"], 1)
                if v == 6:
                    wait(pe, "xT_made", g + 1)
                    for b in range(PAIR):
                        for c in range(KC):
                            cols = xT[:, c, b * L:(b + 1) * L]
                            nc.tensor.matmul(g0[:, b * L:(b + 1) * L], wi_rep[:, c, :], cols,
                                             start=(c == 0), stop=False)
                            mm = nc.tensor.matmul(g0[:, b * L:(b + 1) * L], cols, wj_rep[:, c, :],
                                                  start=False, stop=(c == KC - 1))
                    mm.then_inc(S["e_mm"], 1)
                if v == 11:
                    wait(pe, "alpha_made", g + 1)
                    wait(pe, "xnT_made", g)
                    for b in range(PAIR):
                        nc.tensor.matmul(g0[:, b * DIM:(b + 1) * DIM], att[:, b, :], xn[:, b, :],
                                         start=True, stop=True)
                    for b in range(PAIR):
                        mm = nc.tensor.matmul(g1[:, b:b + 1], att[:, b, :], one_col[:, 0:1], start=True, stop=True)
                    mm.then_inc(S["u1_mm"], 1)
                if v == 13:
                    wait(pe, "rinv_made", g + 1)
                    for c in range(KC):
                        for b in range(PAIR):
                            mm = nc.tensor.matmul(g1[:, c * T + b * L:c * T + (b + 1) * L],
                                                  xn[:, b, c * P:(c + 1) * P], att[:, b, :], start=True, stop=True)
                    mm.then_inc(S["u1T_mm"], 1)
                if v == 15:
                    wait(pe, "x1k_made", g + 1)
                    for c in range(KC):
                        for b in range(PAIR):
                            mm = nc.tensor.matmul(g0[:, c * T + b * L:c * T + (b + 1) * L],
                                                  x1k[:, b, c * P:(c + 1) * P], att[:, b, :], start=True, stop=True)
                    mm.then_inc(S["u2T_mm"], 1)
                if v in (16, 18):
                    b = int(v == 18)
                    if b == 0:
                        wait(pe, "u1T_made", g + 1)
                        nc.tensor.matmul(g1[:, :], ones3, bk_row, start=True, stop=False, skip_group_check=True)
                    for c in range(KC):
                        mm = nc.tensor.matmul(g1[:, b * DIM:(b + 1) * DIM], xT[:, c, b * L:(b + 1) * L],
                                              wks[:, 0, c, :], start=False, stop=(c == KC - 1),
                                              skip_group_check=True)
                    if b == 1:
                        mm.then_inc(S["h0_mm"], 1)
                if v in (18, 20, 22):
                    wait(pe, "u2T_made", g + 1)
                    for b, n in {18: [(0, 0)], 20: [(0, 1), (1, 0)], 22: [(1, 1)]}[v]:
                        for c in range(KC):
                            mm = nc.tensor.matmul(g0[:, b * DIM:(b + 1) * DIM],
                                                  (u1T, u2T)[n][:, c, b * L:(b + 1) * L], wks[:, 1 + n, c, :],
                                                  start=(n == 0 and c == 0), stop=(n == 1 and c == KC - 1))
                    if v == 22:
                        mm.then_inc(S["h_mm"], 1)

            def tail(pe, k, p):
                for v in range(Q + 2):
                    project_out(pe, k, p, v)
                    if v < PE_LAG:
                        state_sum(pe, k - 1, 1 - p, v + U - PE_LAG)

            walk(pe, body, tail)

        @block.vector
        def _(dve):
            nc.vector.memset(one_col[:, :], 1.0)
            nc.vector.memset(ones3, 1.0)
            nc.vector.memset(one1, 1.0)
            nc.vector.memset(halfs[:, :], -0.5).then_inc(S["memsets"], 1)
            nc.vector.memset(dec[:, :, :, :], 0.0)
            nc.vector.memset(upad[:, :, :, :], 0.0).then_inc(S["memsets"], 1)
            dve.wait_ge(S["w_graph"], 16 * len(GRAPH_LOADS))
            nc.vector.tensor_copy(s_awrep, s_aw[:, :, None].to_broadcast([P, 2 * KC, P])).then_inc(S["reps_made"], 1)
            nc.vector.tensor_copy(s_bvrep, s_bv[:, :, None].to_broadcast([P, KC, P])).then_inc(S["reps_made"], 1)

            def inject(dve, k, p, v):
                j, q, sl = v // Q, v % Q, v % SLOTS
                if v == 0:
                    wait(dve, "b_loaded", 16 * k + 16)
                if q == 0:
                    wait(dve, "du_made", J * k + j + 1)
                wait(dve, "summed", U * k + v + 1 - SLOTS)
                nc.vector.tensor_tensor(st[:, sl, :, :], du[:, p, j, None, :].to_broadcast([P, SU, T]),
                                        bc[:, p, 0, SU * q:SU * q + SU, :], ALU.mult).then_inc(S["injected"], 1)

            def scan_unit(dve, k, p, v):
                sl = v % SLOTS
                wait(dve, "decays", U * k + v + 1)
                wait(dve, "injected", U * k + v + 1)
                flat = st[:, sl, :, :].rearrange("p s t -> p (s t)")
                nc.vector.tensor_tensor_scan(flat, dec[:, sl, :, :].rearrange("p s t -> p (s t)"), flat, 0.0,
                                             ALU.mult, ALU.add).then_inc(S["scanned"], 1)

            def skip_term(dve, k, p, v):
                if v % Q != 2:
                    return
                j = v // Q - 1
                if j < 0:
                    if not has_previous(k):
                        return
                    k, p, j = k - 1, 1 - p, J - 1
                wait(dve, "summed", U * k + Q * (j + 1))
                wait(dve, "y_gated", J * k + j - 1)
                nc.vector.scalar_tensor_tensor(yv[:, j % 2, :], u[:, p, j, :], chan[:, TAPS + 2, j:j + 1],
                                               y_ps[:, j % 2, 0:T], ALU.mult, ALU.add).then_inc(S["y_skip"], 1)

            def finish(dve, k):
                wait(dve, "out_mm", J * k + J)
                wait(dve, "x1_reloaded", 16 * k + 16)
                nc.vector.tensor_tensor(last_x[:, :, :], o_ps[:, :, :], last_x[:, :, :], ALU.add)\
                    .then_inc(S["finished"], 1)

            def tap(dve, g, r, v, second):
                if not 2 <= v < 2 * J + 2:
                    return
                j = v // 2 - 1
                m = 2 * (v % 2) + second
                n = (TAPS - 1) * (J * g + j) + m
                if m == TAPS - 1:
                    return
                dst = u[:, r, j, :].rearrange("p (b t) -> p b t", b=PAIR)
                if m == 0:
                    wait(dve, "u_biased", J * g + j + 1)
                else:
                    wait(dve, "taps", n)
                nc.vector.scalar_tensor_tensor(dst, upad[:, j % 2, :, m:m + L], chan[:, m, j:j + 1], dst,
                                               ALU.mult, ALU.add).then_inc(S["taps"], 1)

            def graph_dve(dve, g, v, late):
                if (v, late) in ((1, 0), (25, 0)):
                    second = v == 25
                    if second:
                        wait(dve, "x1_made", g + 1)
                    else:
                        wait(dve, "x_loaded", 16 * g + 16)
                    for b in range(PAIR):
                        a = nc.vector.bn_stats(bstat[:, b, :], xg[:, b, :])
                    a.then_inc(S["stats"], 1)
                if (v, late) in ((1, 1), (25, 1)):
                    second = v == 25
                    wait(dve, "stats", 2 * g + 1 + second)
                    stand(dve)
                    for b in range(PAIR):
                        a = nc.vector.bn_aggr(mv[:, b, :], bstat[:, b, :])
                    a.then_inc(S["aggr"], 1)
                if (v, late) in ((3, 0), (27, 0)):
                    second = v == 27
                    wait(dve, "rstd_made", 2 * g + 1 + second)
                    if second:
                        wait(dve, "h_mm", g + 1)
                    else:
                        wait(dve, "transposed", 2 * g)
                    for b in range(PAIR):
                        a = nc.vector.tensor_scalar(xn[:, b, :], xg[:, b, :], mv[:, b, 0:1], rstd[:, b:b + 1],
                                                    ALU.subtract, ALU.mult)
                    a.then_inc(S["normed"], 1)
                if (v, late) == (8, 0):
                    wait(dve, "e_biased", g + 1)
                    nc.vector.scalar_tensor_tensor(att[:, :, :], att[:, :, :], 0.2, att[:, :, :],
                                                   ALU.mult, ALU.max).then_inc(S["e_leaky"], 1)
                if (v, late) == (10, 0):
                    wait(dve, "e_exp", g + 1)
                    wait(dve, "adj_loaded", 16 * g + 16)
                    nc.vector.tensor_tensor(att[:, :, :], att[:, :, :], adjt[:, :, :], ALU.mult)\
                        .then_inc(S["alpha_made"], 1)
                if (v, late) == (12, 0):
                    wait(dve, "u1_mm", g + 1)
                    nc.vector.tensor_scalar(rowsum[:, :], g1[:, 0:PAIR], EPS_ROW, None, ALU.add)\
                        .then_inc(S["rowsum_eps"], 1)
                    wait(dve, "rowsum_eps", g + 1)
                    nc.vector.reciprocal(rinv[:, :], rowsum[:, :]).then_inc(S["rinv_made"], 1)
                if (v, late) == (24, 0):
                    wait(dve, "h0_made", g + 1)
                    wait(dve, "h_mm", g + 1)
                    for b in range(PAIR):
                        a = nc.vector.scalar_tensor_tensor(x1k[:, b, :], g0[:, b * DIM:(b + 1) * DIM],
                                                           rinv[:, b:b + 1], x1k[:, b, :], ALU.mult, ALU.add)
                    a.then_inc(S["h_summed"], 1)
                if (v, late) == (24, 1):
                    wait(dve, "h_summed", g + 1)
                    nc.vector.scalar_tensor_tensor(xg[:, :, :], x1k[:, :, :], 0.0, xg[:, :, :],
                                                   ALU.max, ALU.add).then_inc(S["x1_made"], 1)

            def body(dve, k, p, scan, dense, ends, begins):
                r = 1 - p
                if dense and not scan:
                    dve.wait_ge(S["decay_exp"], 1)
                    nc.vector.tensor_scalar(decay[:, :, :], decay[:, :, :], -1.0, None, ALU.mult)\
                        .then_inc(S["decay_neg"], 1)
                    dve.wait_ge(S["folded"], FOLDS + 1)
                    nc.vector.tensor_tensor(bconv[:, :], bxz[:, 0:J], chan[:, TAPS - 1, :], ALU.mult)\
                        .then_inc(S["bconv_made"], 1)
                    dve.wait_ge(S["bconv_made"], 1)
                    nc.vector.tensor_tensor(bconv[:, :], bconv[:, :], chan[:, TAPS, :], ALU.add)\
                        .then_inc(S["bconv_made"], 1)
                if scan:
                    inject(dve, k, p, 0)
                for v in range(U):
                    if dense:
                        tap(dve, k + 1, r, v, 0)
                    if scan and v + 1 < U:
                        inject(dve, k, p, v + 1)
                    if dense:
                        tap(dve, k + 1, r, v, 1)
                    gs = graph_step(k, p, v, ends, begins)
                    if gs:
                        graph_dve(dve, gs[0], gs[2], 0)
                    if scan:
                        scan_unit(dve, k, p, v)
                        skip_term(dve, k, p, v)
                        if v == 7 and has_previous(k):
                            finish(dve, k - 1)
                    if gs:
                        graph_dve(dve, gs[0], gs[2], 1)

            def tail(dve, k, p):
                skip_term(dve, k, p, 2)
                finish(dve, k - 1)

            walk(dve, body, tail)


def kernel(**inputs):
    import numpy as np
    import concourse.bacc as bacc
    from concourse.bass_utils import run_bass_kernel_spmd

    a = {n: np.asarray(v) for n, v in inputs.items()}

    def chunks(w):
        return w.reshape(w.shape[0] // P, P, *w.shape[1:]).swapaxes(0, 1)

    g, f = "L0_gnn_", "L0_ffn_"
    ins = {
        "x": a["x"], "adjT": a["adj"].swapaxes(1, 2),
        "w_inT": chunks(a[f + "W_in"].T), "w_fc1": chunks(a[f + "W_fc1"]),
        "w_out": chunks(a[f + "W_out"]), "w_fc2T": chunks(a[f + "W_fc2"].T),
        "w_vT": chunks(a[g + "Wv"].T), "aw": chunks(a[g + "aw"][:, 0]), "bv": chunks(a[g + "bv"]),
        "ab": a[g + "ab"].reshape(1, 1), "wk": a[g + "Wk"].reshape(HOPS, KC, P, DIM).transpose(2, 0, 1, 3),
        "bk": a[g + "bk"], "b_fc1": chunks(a[f + "b_fc1"]),
        "conv_w": chunks(a[f + "conv_w"]).swapaxes(1, 2), "conv_b": chunks(a[f + "conv_b"]),
        "w_xT": chunks(a[f + "W_xproj"].T), "w_dtT": a[f + "W_dt"].T, "b_dt": chunks(a[f + "b_dt"]),
        "a_log": chunks(a[f + "A_log"]), "skip": chunks(a[f + "D"]), "b_fc2": a[f + "b_fc2"].reshape(1, DIM),
        "ident_in": np.eye(P, dtype=np.float32),
    }
    nc = bacc.Bacc("TRN2", target_bir_lowering=False, num_devices=1, dynamic_dma_scratch_size=1024)
    arrays, args = {}, {}
    for name, v in ins.items():
        v = np.ascontiguousarray(v)
        arrays[name + "_dram"] = v
        args[name] = nc.dram_tensor(name + "_dram", v.shape, mybir.dt.from_np(v.dtype), kind="ExternalInput").ap()
    out = nc.dram_tensor("out_dram", (BATCH, L, DIM), F32, kind="ExternalOutput").ap()
    build(nc, **args, out=out)
    r = run_bass_kernel_spmd(nc, [arrays], core_ids=[0])
    return r.results[0]["out_dram"]
```
